# Optimizing a Trainium2 kernel written in Bass

```python
import numpy as np
import jax
import jax.numpy as jnp

def _softmax(x, axis=-1):
    return jax.nn.softmax(x, axis=axis)

def _gelu(x):
    return jax.nn.gelu(x, approximate=True)

def _silu(x):
    return jax.nn.silu(x)

def _sigmoid(x):
    return jax.nn.sigmoid(x)

def _layernorm(x, axis=-1, eps=1e-05):
    m = jnp.mean(x, axis=axis, keepdims=True)
    v = jnp.var(x, axis=axis, keepdims=True)
    return (x - m) / jnp.sqrt(v + eps)

def _scatter_add(tgt, idx, src, axis=0):
    return tgt.at[idx].add(src)

def _segment_sum(src, seg, n):
    return jax.ops.segment_sum(src, seg, n)
kernel_name = 'mk_gnn_ffn_d1_gnn_r16_67a032'

def setup_inputs(seed: int=0):
    np.random.seed(seed)
    _w = jnp.asarray

    def _rec_inputs():
        import jax
        import jax.numpy as jnp
        _gk = jax.random.key(seed)
        x = -0.0006008 + 1.001 * jax.random.normal(jax.random.fold_in(_gk, 1), (3125, 256), jnp.float32)
        src = jax.random.randint(jax.random.fold_in(_gk, 2), (100000,), 0, 3125, jnp.int32)
        dst = jnp.minimum((3125 * jax.random.uniform(jax.random.fold_in(_gk, 3), (100000,)) ** 2.0).astype(jnp.int32), 49999)
        _o = jnp.argsort(dst, stable=True)
        src = src[_o]
        dst = dst[_o]
        edge_type_2 = jax.random.randint(jax.random.fold_in(_gk, 12), (100000,), 0, 2, jnp.int32)
        return (x, src, dst, edge_type_2)
    x, src, dst, edge_type_2 = _rec_inputs()

    def _L0_gnn_setup():
        import jax, jax.numpy as jnp
        import numpy as np
        N_NODES = 625
        N_EDGES = 20000
        D = 256
        D_OUT = 256
        NUM_REL = 2
        key = jax.random.key(seed)
        ks = jax.random.split(key, 16)
        s = 1.0 / np.sqrt(D)
        inp = {}
        inp['feat'] = jax.random.normal(ks[0], (N_NODES, D), dtype=jnp.float32)
        inp['src'] = jax.random.randint(ks[1], (N_EDGES,), 0, N_NODES, dtype=jnp.int32)
        inp['dst'] = jax.random.randint(ks[2], (N_EDGES,), 0, N_NODES, dtype=jnp.int32)
        inp['rel'] = jax.random.randint(ks[3], (N_EDGES,), 0, NUM_REL, dtype=jnp.int32)
        inp['W_rel'] = jax.random.normal(ks[4], (NUM_REL, D, D), dtype=jnp.float32) * s
        inp['b_rel'] = jax.random.normal(ks[5], (NUM_REL, D), dtype=jnp.float32) * s
        inp['W_ih'] = jax.random.normal(ks[6], (4 * D, D), dtype=jnp.float32) * s
        inp['b_ih'] = jax.random.normal(ks[7], (4 * D,), dtype=jnp.float32) * s
        inp['b_hh'] = jax.random.normal(ks[8], (4 * D,), dtype=jnp.float32) * s
        h = D // 2
        inp['W1'] = jax.random.normal(ks[9], (h, D), dtype=jnp.float32) * s
        inp['b1'] = jax.random.normal(ks[10], (h,), dtype=jnp.float32) * s
        inp['W2'] = jax.random.normal(ks[11], (h, h), dtype=jnp.float32) * (1.0 / np.sqrt(h))
        inp['b2'] = jax.random.normal(ks[12], (h,), dtype=jnp.float32) * (1.0 / np.sqrt(h))
        inp['W3'] = jax.random.normal(ks[13], (D_OUT, h), dtype=jnp.float32) * (1.0 / np.sqrt(h))
        inp['b3'] = jax.random.normal(ks[14], (D_OUT,), dtype=jnp.float32) * (1.0 / np.sqrt(h))
        return inp
    _L0_gnn_all = _L0_gnn_setup()
    _L0_gnn_in = {k: v for k, v in _L0_gnn_all.items() if k in ('W_rel', 'b_rel', 'W_ih', 'b_ih', 'b_hh', 'W1', 'b1', 'W2', 'b2', 'W3', 'b3')}
    del _L0_gnn_all

    def _L0_ffn_setup():
        import jax, jax.numpy as jnp
        import numpy as np
        B, S, D = (8, 256, 256)
        H = 4 * D
        CAPACITY = 0.5
        key = jax.random.key(seed)
        ks = jax.random.split(key, 6)
        x = jax.random.normal(ks[0], (B, S, D), dtype=jnp.float32)
        attention_mask = jnp.zeros((B, 1, 1, S), dtype=jnp.float32)
        wr = jax.random.normal(ks[1], (D, 1), dtype=jnp.float32) * 0.02
        br = jnp.zeros((1,), dtype=jnp.float32)
        w1 = jax.random.normal(ks[2], (D, H), dtype=jnp.float32) * 0.02
        b1 = jnp.zeros((H,), dtype=jnp.float32)
        w2 = jax.random.normal(ks[3], (H, D), dtype=jnp.float32) * 0.02
        b2 = jnp.zeros((D,), dtype=jnp.float32)
        return {'x': x, 'attention_mask': attention_mask, 'wr': wr, 'br': br, 'w1': w1, 'b1': b1, 'w2': w2, 'b2': b2}
    _L0_ffn_all = _L0_ffn_setup()
    _L0_ffn_in = {k: v for k, v in _L0_ffn_all.items() if k in ('attention_mask', 'wr', 'br', 'w1', 'b1', 'w2', 'b2')}
    del _L0_ffn_all
    return {'x': x, 'src': src, 'dst': dst, 'edge_type_2': edge_type_2, 'L0_gnn_W_rel': _L0_gnn_in['W_rel'], 'L0_gnn_b_rel': _L0_gnn_in['b_rel'], 'L0_gnn_W_ih': _L0_gnn_in['W_ih'], 'L0_gnn_b_ih': _L0_gnn_in['b_ih'], 'L0_gnn_b_hh': _L0_gnn_in['b_hh'], 'L0_gnn_W1': _L0_gnn_in['W1'], 'L0_gnn_b1': _L0_gnn_in['b1'], 'L0_gnn_W2': _L0_gnn_in['W2'], 'L0_gnn_b2': _L0_gnn_in['b2'], 'L0_gnn_W3': _L0_gnn_in['W3'], 'L0_gnn_b3': _L0_gnn_in['b3'], 'L0_ffn_attention_mask': _L0_ffn_in['attention_mask'], 'L0_ffn_wr': _L0_ffn_in['wr'], 'L0_ffn_br': _L0_ffn_in['br'], 'L0_ffn_w1': _L0_ffn_in['w1'], 'L0_ffn_b1': _L0_ffn_in['b1'], 'L0_ffn_w2': _L0_ffn_in['w2'], 'L0_ffn_b2': _L0_ffn_in['b2']}

def reference(x, src, dst, edge_type_2, L0_gnn_W_rel, L0_gnn_b_rel, L0_gnn_W_ih, L0_gnn_b_ih, L0_gnn_b_hh, L0_gnn_W1, L0_gnn_b1, L0_gnn_W2, L0_gnn_b2, L0_gnn_W3, L0_gnn_b3, L0_ffn_attention_mask, L0_ffn_wr, L0_ffn_br, L0_ffn_w1, L0_ffn_b1, L0_ffn_w2, L0_ffn_b2):
    import jax
    import jax.numpy as jnp

    def _L0_gnn_ref(feat, src, dst, rel, W_rel, b_rel, W_ih, b_ih, b_hh, W1, b1, W2, b2, W3, b3):
        import jax, jax.numpy as jnp
        import numpy as np
        N_NODES = 625
        N_EDGES = 20000
        D = 256
        D_OUT = 256
        NUM_REL = 2
        n_nodes = feat.shape[0]
        S = feat[src]

        def edge_nn(x, W, b):
            h = jax.nn.relu(x @ W.T + b)
            return jax.nn.relu(h @ W.T + b)
        msgs = jnp.zeros_like(S)
        for r in range(W_rel.shape[0]):
            msgs = jnp.where((rel == r)[:, None], edge_nn(S, W_rel[r], b_rel[r]), msgs)
        agg = jax.ops.segment_sum(msgs, dst, num_segments=n_nodes)
        gates = agg @ W_ih.T + b_ih + b_hh
        i, f, g, o = jnp.split(gates, 4, axis=-1)
        c = jax.nn.sigmoid(i) * jnp.tanh(g)
        hn = jax.nn.sigmoid(o) * jnp.tanh(c)
        x = jax.nn.relu(hn @ W1.T + b1)
        x = jax.nn.relu(x @ W2.T + b2)
        return x @ W3.T + b3

    def _L0_ffn_ref(x, attention_mask, wr, br, w1, b1, w2, b2):
        import jax, jax.numpy as jnp
        import numpy as np
        B, S, D = (8, 256, 256)
        H = 4 * D
        CAPACITY = 0.5
        b, s, d = x.shape
        weights = (jnp.einsum('bsd,do->bso', x, wr) + br)[..., 0]
        k = max(1, int(CAPACITY * s))
        kk = k - 1 if k > 1 else 1
        _, idx = jax.lax.top_k(weights, k)
        sel_idx = idx[:, :kk]
        sel = jnp.take_along_axis(x, sel_idx[:, :, None], axis=1)
        h = jax.nn.gelu(jnp.einsum('bkd,dh->bkh', sel, w1) + b1)
        y = jnp.einsum('bkh,hd->bkd', h, w2) + b2
        w_sel = jnp.take_along_axis(weights, sel_idx, axis=1)
        y = y * w_sel[..., None]
        batch_idx = jnp.arange(b)[:, None]
        processed = jnp.zeros_like(x).at[batch_idx, sel_idx].set(y)
        return processed + x
    x = x + _L0_gnn_ref(_layernorm(x, axis=-1), src, dst, edge_type_2, L0_gnn_W_rel, L0_gnn_b_rel, L0_gnn_W_ih, L0_gnn_b_ih, L0_gnn_b_hh, L0_gnn_W1, L0_gnn_b1, L0_gnn_W2, L0_gnn_b2, L0_gnn_W3, L0_gnn_b3)
    x = x + _L0_ffn_ref(_layernorm(x, axis=-1)[None], L0_ffn_attention_mask, L0_ffn_wr, L0_ffn_br, L0_ffn_w1, L0_ffn_b1, L0_ffn_w2, L0_ffn_b2)[0]
    return x

_drawn_inputs = setup_inputs


def setup_inputs(seed=0):
    import zlib

    import numpy as np

    out = dict(_drawn_inputs(seed))
    spreads = {'L0_ffn_b1': (0.0, 0.8), 'L0_ffn_b2': (0.0, 0.602)}
    factors = {'L0_gnn_b_ih': 8.0,
     'L0_gnn_b_hh': 8.0,
     'L0_ffn_wr': 3.68,
     'L0_ffn_w1': 3.776,
     'L0_ffn_w2': 3.536}
    for name, (base, spread) in spreads.items():
        noise = np.random.default_rng([zlib.crc32(name.encode()), seed]).standard_normal(out[name].shape)
        drawn = base * np.exp(spread * noise) if base else spread * noise
        out[name] = jnp.asarray(drawn.astype(out[name].dtype))
    for name, factor in factors.items():
        out[name] = (out[name] * factor).astype(out[name].dtype)
    return out
```

```python
from contextlib import ExitStack

import concourse.bass as bass
from concourse import mybir

ALU = mybir.AluOpType
ACT = mybir.ActivationFunctionType
AX = mybir.AxisListType
F32 = mybir.dt.float32
F16 = mybir.dt.float16
I32 = mybir.dt.int32
ds = bass.ds

P = 128
EPS = 1e-5
PAD_DST = 1 << 20


def build(nc, x, src, dst, rel, w_rel_t, b_rel_col, b_rel_row, w_ih_t, b_ih_col, b_hh_col, w1_t, b1_col, w2_t, b2_col,
          w3_t, b3_row, wr_row, br_one, f1, f1_col, f2, f2_row, out):
    N, D = x.shape
    E = src.shape[0]
    H = f1.shape[1]
    KC = D // P
    HC = H // P
    NB = -(-N // P)
    NS = -(-NB // 4)
    LAST = N - (NB - 1) * P
    TE = -(-E // P)
    TC = -(-(TE + 4) // P)
    TW = TC * P
    RQ = 8
    QP = -(-(-(-TE // 4) + 1) // RQ) * RQ
    NSEL = max(1, int(0.5 * N)) - 1
    W = 2 * D
    assert D == 256 and (QP + RQ) * 4 <= TW

    def blocks(s):
        return min(4, NB - 4 * s)

    with ExitStack() as ctx:
        def sb(name, shape, dt=F32):
            return ctx.enter_context(nc.sbuf_tensor(name, shape, dt))

        def sem(name):
            return ctx.enter_context(nc.semaphore(name))

        table = nc.dram_tensor("message_table", [2 * NB * P, W], F16).ap()

        X = sb("X", [P, NB, D])
        Y = sb("Y", [P, NB, D])
        ring = sb("ring", [P, RQ * 4 * W], F16)
        prep = ring[:, :].bitcast(F32)
        raw_i = ring[:, :].bitcast(I32)

        def pv(n, v=prep):
            return v[:, n * TW:(n + 1) * TW]
        src_i, dst_i, rel_i = pv(0, raw_i), pv(1, raw_i), pv(2, raw_i)
        dst_f, row_f = pv(3), pv(4)
        tmin_b, tmax_b = pv(5), pv(6)
        up, down = pv(7), pv(8)
        dstT = sb("dstT", [P, TW])
        rowT = sb("rowT", [P, TW], I32)
        rows4 = sb("rows4", [P, RQ * 4], I32)
        onehot = sb("onehot", [P, 4, P], F16)
        big = sb("big", [P, HC * 512])
        hT = big[:, :].rearrange("p (c n) -> p c n", c=HC)
        h1T = big[:, 0:2048].rearrange("p (r c n) -> p r c n", r=2, c=KC)
        stage = big[:, 2048:4096].bitcast(F16).rearrange("p (b t w) -> p b t w", b=2, t=4)
        w_all = big[:, 0:NB * P]
        fT = sb("fT", [P, KC, 512])
        G = sb("G", [P, 6, 512])
        aggT = sb("aggT", [P, KC, 512])
        hnT = sb("hnT", [P, KC, 512])
        n2 = sb("n2", [P, 4, D])
        agg = sb("agg", [P, 4, D])
        agg_hi = sb("agg_hi", [P, D])
        diag = sb("diag", [P, NB, P])
        WR = sb("WR", [P, 2, KC, D])
        WI = sb("WI", [P, KC, 3 * D])
        W1 = sb("W1", [P, KC, P])
        W2 = sb("W2", [P, P])
        W3 = sb("W3", [P, D])
        F1 = sb("F1", [P, KC, H])
        F2 = sb("F2", [P, HC, D])
        br_col = sb("br_col", [P, 4])
        br_row = sb("br_row", [1, 2 * D])
        bi = sb("bi", [P, 6])
        bh = sb("bh", [P, 6])
        bg = sb("bg", [P, 6])
        b1 = sb("b1", [P, 1])
        b2 = sb("b2", [P, 1])
        b3 = sb("b3", [P, D])
        wr = sb("wr", [P, D])
        br = sb("br", [P, 1])
        fb1 = sb("fb1", [P, HC])
        fb2 = sb("fb2", [P, D])
        ident = sb("ident", [P, P])
        ones = sb("ones", [P, P])
        zeros = sb("zeros", [P, 512], F16)
        iota = sb("iota", [P, P])
        pcol = sb("pcol", [P, 1])
        before = sb("before", [P, P])
        lo_g = sb("lo_g", [32, 1])
        st = sb("st", [P, 4, 6])
        mv = sb("mv", [P, NB, 2])
        ve = sb("ve", [P, NB])
        sd = sb("sd", [P, NB])
        rs = sb("rs", [P, NB])
        wcol = sb("wcol", [P, NB])
        junk = sb("junk", [P, NB * P])
        tmm = sb("tmm", [P, 2, TC])
        rng = sb("rng", [32, 2])
        rows_g = sb("rows_g", [1, 64])
        q_i = sb("q_i", [1, 64], I32)
        q_f = sb("q_f", [1, 64])
        q0, q1 = q_f[:, 0:32], q_f[:, 32:64]
        okv = sb("okv", [1, 32])
        pn = sb("pn", [1, 4, 32])
        pf = sb("pf", [1, 4, 32])
        plan = sb("plan", [1, 4, 32], I32)
        rank4 = sb("rank4", [P, 4, NB])
        rank = sb("rank", [P, NB])
        mw = sb("mw", [P, NB])

        AG = [ctx.enter_context(nc.psum_tensor(f"AG{i}", [P, 512], F32)) for i in range(2)]
        BIG = [ctx.enter_context(nc.psum_tensor(f"BIG{i}", [P, 512], F32)) for i in range(4)]
        SM = [ctx.enter_context(nc.psum_tensor(f"SM{i}", [P, 512], F32)) for i in range(2)]

        x_in = sem("x_in")
        edges_in = sem("edges_in")
        pads_set = sem("pads_set")
        weights_in = sem("weights_in")
        bias_ready = sem("bias_ready")
        consts = sem("consts")
        v_step = sem("v_step")
        feat_ready = sem("feat_ready")
        var_ready = sem("var_ready")
        std_ready = sem("std_ready")
        big_full = sem("big_full")
        big_free = sem("big_free")
        sm_full = sem("sm_full")
        sm_free = sem("sm_free")
        hi_ready = sem("hi_ready")
        stored = [sem(f"stored{i}") for i in range(2)]
        lists_ready = sem("lists_ready")
        diag_ready = sem("diag_ready")
        range_ready = sem("range_ready")
        plan_ready = sem("plan_ready")
        idx_ready = sem("idx_ready")
        idx_seen = sem("idx_seen")
        gathered = [sem(f"gathered{i}") for i in range(RQ)]
        landed = sem("landed")
        released = sem("released")
        oh_ready = [sem(f"oh_ready{i}") for i in range(2)]
        oh_used = [sem(f"oh_used{i}") for i in range(2)]
        agg_full = sem("agg_full")
        agg_copied = sem("agg_copied")
        agg_done = sem("agg_done")
        c_ready = sem("c_ready")
        tc_ready = sem("tc_ready")
        hn_ready = sem("hn_ready")
        n2_ready = sem("n2_ready")
        out_ready = sem("out_ready")
        out_done = sem("out_done")

        big_items, sm_items, at = [], [], {}

        def note(kind, key):
            lst = big_items if kind == "big" else sm_items
            at[(kind,) + key] = len(lst)
            lst.append(key)

        def order():
            def turn(s):
                for c in range(KC):
                    note("big", ("featT", s, c))
            turn(0)
            for s in range(NS):
                for r in range(2):
                    for m in range(KC):
                        note("big", ("L1", s, r, m))
                if s + 1 < NS:
                    turn(s + 1)
                for r in range(2):
                    for j in range(blocks(s)):
                        note("sm", ("L2", s, r, j))
                if s == 1:
                    for n in range(4):
                        note("big", ("lists", n))
                    for n in range(4):
                        note("big", ("spread", n))
                    note("sm", ("ranges",))
            for s, ph in phases():
                n = blocks(s)
                if ph == 0:
                    for c in range(KC):
                        note("big", ("aggT", s, c))
                    for g in range(6):
                        note("big", ("gate", s, g))
                elif ph == 1:
                    note("big", ("W1", s))
                    note("big", ("W2", s))
                    for j in range(n):
                        note("sm", ("W3", s, j))
                elif ph == 2:
                    for c in range(KC):
                        note("big", ("n2T", s, c))
                    for c in range(HC):
                        note("big", ("F1", s, c))
                else:
                    for j in range(n):
                        note("sm", ("F2", s, j))
            for n in range(NS):
                note("big", ("wrow", n))

        def phases():
            return [(s, ph) for s in range(NS) for ph in range(4)]

        def after_block(b):
            if b == NB - 1:
                return [p for p in phases() if 4 * (p[0] + 1) + p[1] >= b]
            return [p for p in phases() if 4 * (p[0] + 1) + p[1] == b]

        order()

        def items(kind, first):
            return at[(kind,) + first]

        block = ctx.enter_context(nc.Block())

        @block.sync
        def _(sp):
            for n in range(0, NB - 1, 8):
                sp.dma_start(X[:, n:n + 8, :], x[n * P:(n + 8) * P, :].rearrange("(t p) d -> p t d", p=P)).then_inc(x_in, 16)
            sp.wait_ge(pads_set, 1)
            sp.dma_start(X[0:LAST, NB - 1, :], x[(NB - 1) * P:N, :]).then_inc(x_in, 16)
            full = E // P
            wide = full // P
            sp.wait_ge(pads_set, 4)
            for a, t in ((src, src_i), (dst, dst_i), (rel, rel_i)):
                t3 = t.rearrange("p (c e) -> p c e", c=TC)
                sp.dma_start(t3[:, 0:wide, :], a[0:wide * P * P].rearrange("(c p e) -> p c e", p=P, e=P)).then_inc(edges_in, 16)
                if full > wide * P:
                    sp.dma_start(t3[0:full - wide * P, wide, :],
                                 a[wide * P * P:full * P].rearrange("(p e) -> p e", e=P)).then_inc(edges_in, 16)
                if E > full * P:
                    sp.dma_start(t3[full - wide * P:full - wide * P + 1, wide, 0:E - full * P],
                                 a[full * P:E].rearrange("(p e) -> p e", p=1)).then_inc(edges_in, 16)
            for s in range(NS):
                n = blocks(s)
                for r in range(2):
                    k = 2 * s + r
                    sp.wait_ge(sm_free, items("sm", ("L2", s, r, n - 1)) + 1)
                    row = (r * NB + 4 * s) * P
                    sp.dma_start(table[row:row + n * P, :].rearrange("(t p) w -> p t w", p=P),
                                 stage[:, k % 2, 0:n, :]).then_inc(stored[k % 2], 16)
            sp.wait_ge(plan_ready, 1)
            quads = sp.value_load(plan[0:1, 3, 0:1], min_val=1, max_val=QP)
            passes = sp.value_load(plan[0:1, 3, 2:3], min_val=1, max_val=NB)
            want = sp.alloc_register("want")
            sp.reg_mov(want, 64)
            with sp.Fori(0, passes):
                with sp.Fori(0, quads, RQ):
                    w = sp.snap(want)
                    for j in range(RQ):
                        sp.wait_ge(gathered[j], w)
                        sp.sem_inc(landed, 1)
                    sp.reg_add(want, want, 64)
            for n in range(NB):
                sp.wait_ge(out_ready, n + 1)
                if n < NB - 1:
                    sp.dma_start(out[n * P:(n + 1) * P, :], X[:, n, :]).then_inc(out_done, 16)
                else:
                    sp.dma_start(out[n * P:N, :], X[0:LAST, n, :]).then_inc(out_done, 16)
            sp.wait_ge(out_done, 16 * NB)

        @block.gpsimd
        def _(pool):
            nc.gpsimd.memset(X[:, NB - 1, :], 0.0).then_inc(pads_set, 1)
            nc.gpsimd.memset(src_i, 0).then_inc(pads_set, 1)
            nc.gpsimd.memset(rel_i, 0).then_inc(pads_set, 1)
            nc.gpsimd.memset(dst_i, PAD_DST).then_inc(pads_set, 1)
            nc.gpsimd.iota(iota[:, :], pattern=[[1, P]], base=0, channel_multiplier=0,
                           allow_small_or_imprecise_dtypes=True).then_inc(consts, 1)
            nc.gpsimd.iota(pcol[:, :], pattern=[[1, 1]], base=0, channel_multiplier=1,
                           allow_small_or_imprecise_dtypes=True).then_inc(consts, 1)
            nc.gpsimd.memset(ones[:, :], 1.0).then_inc(consts, 1)
            nc.gpsimd.memset(zeros[:, :], 0.0).then_inc(consts, 1)
            nc.gpsimd.iota(up, pattern=[[1, TW]], base=0, channel_multiplier=0,
                           allow_small_or_imprecise_dtypes=True).then_inc(consts, 1)
            nc.gpsimd.iota(down, pattern=[[-1, TW]], base=TW - 1, channel_multiplier=0,
                           allow_small_or_imprecise_dtypes=True).then_inc(consts, 1)
            nc.gpsimd.iota(lo_g[:, :], pattern=[[1, 1]], base=0, channel_multiplier=P,
                           allow_small_or_imprecise_dtypes=True).then_inc(consts, 1)
            nc.gpsimd.memset(pf[:, 0, :], float(QP - 1)).then_inc(consts, 1)
            nc.gpsimd.memset(pf[:, 1, :], 0.0).then_inc(consts, 1)
            nc.gpsimd.memset(pf[:, 2, :], float(QP)).then_inc(consts, 1)
            nc.gpsimd.memset(pf[:, 3, :], float(NB)).then_inc(consts, 1)
            pool.wait_ge(consts, 11)
            nc.gpsimd.memset(pf[:, 0, 0:1], 0.0).then_inc(consts, 1)
            nc.gpsimd.memset(pf[:, 1, 0:1], 1.0).then_inc(consts, 1)
            nc.gpsimd.memset(pf[:, 2, 0:1], float(QP - 1)).then_inc(consts, 1)
            nc.gpsimd.memset(pf[:, 3, 0:1], float(QP)).then_inc(consts, 1)
            nc.gpsimd.memset(pf[:, 3, 1:2], 0.0).then_inc(consts, 1)

            pool.wait_ge(plan_ready, 1)
            quads = pool.value_load(plan[0:1, 3, 0:1], min_val=1, max_val=QP)
            first = pool.value_load(plan[0:1, 3, 1:2], min_val=0, max_val=QP - 1)
            passes = pool.value_load(plan[0:1, 3, 2:3], min_val=1, max_val=NB)
            for k in range(2):
                pool.wait_ge(stored[k], 16 * NS)
            pos = pool.alloc_register("pos")
            col = pool.alloc_register("col")
            pool.reg_mov(pos, 0)
            with pool.Fori(0, passes):
                pool.reg_mul(col, first, 4)
                with pool.Fori(0, quads, RQ):
                    p0 = pool.snap(pos, min_val=0, max_val=NB * QP)
                    c0 = pool.snap(col, min_val=0, max_val=QP * 4)
                    for j in range(RQ):
                        pool.wait_ge(released, p0 + (j + 1))
                        nc.gpsimd.tensor_copy(rows4[:, 4 * j:4 * j + 4], rowT[:, ds(c0 + 4 * j, 4)]).then_inc(idx_ready, 1)
                        pool.wait_ge(idx_ready, p0 + (j + 1))
                        pool.sem_inc(idx_seen, 1)
                        for i in range(4):
                            k = 4 * j + i
                            nc.gpsimd.indirect_dma_start(
                                ring[:, k * W:(k + 1) * W], None, table,
                                bass.IndirectOffsetOnAxis(ap=rows4[:, k:k + 1], axis=0)).then_inc(gathered[j], 16)
                    pool.reg_add(pos, pos, RQ)
                    pool.reg_add(col, col, 4 * RQ)

        @block.scalar
        def _(act):
            loads = [(WR[:, :, :, :], w_rel_t.rearrange("r (c p) n -> p r c n", p=P)),
                     (br_col[:, :], b_rel_col), (br_row[:, :], b_rel_row),
                     (WI[:, :, :], w_ih_t.rearrange("(c p) n -> p c n", p=P)),
                     (bi[:, :], b_ih_col), (bh[:, :], b_hh_col),
                     (W1[:, :, :], w1_t.rearrange("(c p) n -> p c n", p=P)), (b1[:, :], b1_col),
                     (W2[:, :], w2_t), (b2[:, :], b2_col), (W3[:, :], w3_t),
                     (b3[:, :], b3_row.broadcast_to([P, D])), (wr[:, :], wr_row.broadcast_to([P, D])),
                     (br[:, :], br_one.broadcast_to([P, 1])),
                     (F1[:, :, :], f1.rearrange("(c p) n -> p c n", p=P)), (fb1[:, :], f1_col),
                     (F2[:, :, :], f2.rearrange("(c p) n -> p c n", p=P)), (fb2[:, :], f2_row.broadcast_to([P, D]))]
            assert len(loads) == N_LOADS
            for t, a in loads:
                act.dma_start(t, a).then_inc(weights_in, 16)
            act.wait_ge(weights_in, 16 * N_LOADS)

            def big(*key):
                n = at[("big",) + key]
                act.wait_ge(big_full, n + 1)
                return BIG[n % 4]

            def roots(n, lo, hi):
                act.wait_ge(var_ready, n)
                nc.scalar.activation(sd[:, lo:hi], ve[:, lo:hi], ACT.Sqrt).then_inc(std_ready, 1)

            def turn(s):
                for c in range(KC):
                    b = big("featT", s, c)
                    n = blocks(s) * P
                    nc.scalar.activation(fT[:, c, 0:n], b[:, 0:n], ACT.Copy).then_inc(big_free, 1)

            roots(1, 0, NB)
            turn(0)
            for s in range(NS):
                n = blocks(s) * P
                for r in range(2):
                    for m in range(KC):
                        b = big("L1", s, r, m)
                        nc.scalar.activation(h1T[:, r, m, 0:n], b[:, 0:n], ACT.Relu,
                                             bias=br_col[:, 2 * r + m:2 * r + m + 1]).then_inc(big_free, 1)
                if s + 1 < NS:
                    turn(s + 1)
                for r in range(2):
                    k = 2 * s + r
                    if k >= 2:
                        act.wait_ge(stored[k % 2], 16 * (k // 2))
                    for j in range(blocks(s)):
                        i = at[("sm", "L2", s, r, j)]
                        act.wait_ge(sm_full, i + 1)
                        nc.scalar.activation(stage[:, k % 2, j, 0:D], SM[i % 2][:, 0:D], ACT.Relu).then_inc(hi_ready, 1)
                if s == 1:
                    for i in range(4):
                        b = big("lists", i)
                        w = min(4, TC - 4 * (i % 2)) * P
                        o = (i % 2) * 4 * P
                        nc.scalar.activation((dstT if i < 2 else rowT)[:, o:o + w], b[:, 0:w], ACT.Copy).then_inc(big_free, 1)
                    for i in range(4):
                        b = big("spread", i)
                        w = min(4, TC - 4 * (i % 2)) * P
                        o = (i % 2) * 4 * P
                        nc.scalar.activation((tmin_b if i < 2 else tmax_b)[0:32, o:o + w], b[0:32, 0:w],
                                             ACT.Copy).then_inc(big_free, 1)

            def phase(s, ph):
                n = blocks(s) * P
                if ph == 0:
                    for c in range(KC):
                        b = big("aggT", s, c)
                        nc.scalar.activation(aggT[:, c, 0:n], b[:, 0:n], ACT.Copy).then_inc(big_free, 1)
                    for g in range(6):
                        b = big("gate", s, g)
                        nc.scalar.activation(G[:, g, 0:n], b[:, 0:n], ACT.Tanh if g in (2, 3) else ACT.Sigmoid,
                                             bias=bg[:, g:g + 1]).then_inc(big_free, 1)
                    act.wait_ge(c_ready, s + 1)
                    nc.scalar.activation(G[:, 2:4, 0:n], G[:, 0:2, 0:n], ACT.Tanh).then_inc(tc_ready, 1)
                elif ph == 1:
                    b = big("W1", s)
                    nc.scalar.activation(aggT[:, 0, 0:n], b[:, 0:n], ACT.Relu, bias=b1[:, :]).then_inc(big_free, 1)
                    b = big("W2", s)
                    nc.scalar.activation(aggT[:, 1, 0:n], b[:, 0:n], ACT.Relu, bias=b2[:, :]).then_inc(big_free, 1)
                    roots(2 + s, 4 * s, 4 * s + blocks(s))
                elif ph == 2:
                    for c in range(KC):
                        b = big("n2T", s, c)
                        nc.scalar.activation(fT[:, c, 0:n], b[:, 0:n], ACT.Copy).then_inc(big_free, 1)
                    for c in range(HC):
                        b = big("F1", s, c)
                        nc.scalar.activation(hT[:, c, 0:n], b[:, 0:n], ACT.Gelu_apprx_tanh,
                                             bias=fb1[:, c:c + 1]).then_inc(big_free, 1)

            act.wait_ge(bias_ready, 1)
            for b in range(NB):
                act.wait_ge(agg_full, b + 1)
                if b:
                    act.wait_ge(agg_done, b)
                nc.scalar.activation(agg_hi[:, :], AG[b % 2][:, 0:D], ACT.Copy).then_inc(agg_copied, 1)
                for s, ph in after_block(b):
                    phase(s, ph)
            for i in range(NS):
                b = big("wrow", i)
                n = blocks(i) * P
                nc.scalar.activation(w_all[:, 4 * i * P:4 * i * P + n], b[:, 0:n], ACT.Copy).then_inc(big_free, 1)

        @block.tensor
        def _(pe):
            def big(*key):
                n = at[("big",) + key]
                if n >= 4:
                    pe.wait_ge(big_free, n - 3)
                return BIG[n % 4]

            def sm(*key):
                n = at[("sm",) + key]
                if n >= 2:
                    pe.wait_ge(sm_free, n - 1)
                return SM[n % 2]

            def read(*key):
                pe.wait_ge(big_free, at[("big",) + key] + 1)

            def turn(name, s, tile):
                for c in range(KC):
                    b = big(name, s, c)
                    for j in range(blocks(s)):
                        last = nc.tensor.transpose(b[:, j * P:(j + 1) * P], tile(j)[:, c * P:(c + 1) * P], ident[:, :])
                    last.then_inc(big_full, 1)

            def feat(s):
                if s == 0:
                    pe.wait_ge(consts, N_CONSTS)
                pe.wait_ge(feat_ready, s + 1)
                turn("featT", s, lambda j: Y[:, 4 * s + j, :])

            feat(0)
            pe.wait_ge(weights_in, 16 * N_LOADS)
            for s in range(NS):
                n = blocks(s) * P
                read("featT", s, KC - 1)
                for r in range(2):
                    for m in range(KC):
                        b = big("L1", s, r, m)
                        for k in range(KC):
                            last = nc.tensor.matmul(b[:, 0:n], WR[:, r, k, m * P:(m + 1) * P], fT[:, k, 0:n],
                                                    start=(k == 0), stop=(k == KC - 1))
                        last.then_inc(big_full, 1)
                if s + 1 < NS:
                    feat(s + 1)
                for r in range(2):
                    read("L1", s, r, KC - 1)
                    for j in range(blocks(s)):
                        b = sm("L2", s, r, j)
                        for k in range(KC):
                            nc.tensor.matmul(b[:, 0:D], h1T[:, r, k, j * P:(j + 1) * P], WR[:, r, k, :],
                                             start=(k == 0), stop=False)
                        nc.tensor.matmul(b[:, 0:D], ones[0:1, :], br_row[:, r * D:(r + 1) * D],
                                         start=False, stop=True).then_inc(sm_full, 1)
                if s == 1:
                    pe.wait_ge(lists_ready, 1)
                    for i in range(4):
                        b = big("lists", i)
                        for c in range(4 * (i % 2), min(4 * (i % 2) + 4, TC)):
                            last = nc.tensor.transpose(b[:, (c % 4) * P:(c % 4 + 1) * P],
                                                       (dst_f if i < 2 else row_f)[:, c * P:(c + 1) * P], ident[:, :])
                        last.then_inc(big_full, 1)
                    pe.wait_ge(diag_ready, 1)
                    for i in range(4):
                        b = big("spread", i)
                        for c in range(4 * (i % 2), min(4 * (i % 2) + 4, TC)):
                            last = nc.tensor.matmul(b[0:32, (c % 4) * P:(c % 4 + 1) * P], ones[:, 0:32],
                                                    diag[:, (i // 2) * TC + c, :], start=True, stop=True)
                        last.then_inc(big_full, 1)
                    pe.wait_ge(range_ready, 1)
                    b = sm("ranges")
                    nc.tensor.transpose(b[0:1, 0:32], rng[:, 0:1], ident[0:32, 0:32])
                    nc.tensor.transpose(b[0:1, 32:64], rng[:, 1:2], ident[0:32, 0:32]).then_inc(sm_full, 1)

            def phase(s, ph):
                nb = blocks(s)
                n = nb * P
                if ph == 0:
                    pe.wait_ge(agg_done, 4 * s + nb)
                    turn("aggT", s, lambda j: agg[:, j, :])
                    read("aggT", s, KC - 1)
                    for g in range(6):
                        b = big("gate", s, g)
                        for k in range(KC):
                            last = nc.tensor.matmul(b[:, 0:n], WI[:, k, g * P:(g + 1) * P], aggT[:, k, 0:n],
                                                    start=(k == 0), stop=(k == KC - 1))
                        last.then_inc(big_full, 1)
                elif ph == 1:
                    pe.wait_ge(hn_ready, s + 1)
                    b = big("W1", s)
                    for k in range(KC):
                        last = nc.tensor.matmul(b[:, 0:n], W1[:, k, :], hnT[:, k, 0:n], start=(k == 0), stop=(k == KC - 1))
                    last.then_inc(big_full, 1)
                    read("W1", s)
                    b = big("W2", s)
                    nc.tensor.matmul(b[:, 0:n], W2[:, :], aggT[:, 0, 0:n], start=True, stop=True).then_inc(big_full, 1)
                    read("W2", s)
                    for j in range(nb):
                        b = sm("W3", s, j)
                        nc.tensor.matmul(b[:, 0:D], aggT[:, 1, j * P:(j + 1) * P], W3[:, :],
                                         start=True, stop=True).then_inc(sm_full, 1)
                elif ph == 2:
                    pe.wait_ge(n2_ready, s + 1)
                    turn("n2T", s, lambda j: n2[:, j, :])
                    read("n2T", s, KC - 1)
                    for c in range(HC):
                        b = big("F1", s, c)
                        for k in range(KC):
                            last = nc.tensor.matmul(b[:, 0:n], F1[:, k, c * P:(c + 1) * P], fT[:, k, 0:n],
                                                    start=(k == 0), stop=(k == KC - 1))
                        last.then_inc(big_full, 1)
                else:
                    read("F1", s, HC - 1)
                    for j in range(nb):
                        b = sm("F2", s, j)
                        for c in range(HC):
                            last = nc.tensor.matmul(b[:, 0:D], hT[:, c, j * P:(j + 1) * P], F2[:, c, :],
                                                    start=(c == 0), stop=(c == HC - 1))
                        last.then_inc(sm_full, 1)

            pe.wait_ge(plan_ready, 1)
            pos = pe.alloc_register("pe_pos")
            seen = pe.alloc_register("pe_seen")
            pe.reg_mov(pos, 1)
            pe.reg_mov(seen, 1)
            pe.sem_inc(released, RQ)
            pe.sem_inc(oh_used[0], 1)
            pe.sem_inc(oh_used[1], 1)

            def visit(b, release):
                p = pe.snap(pos, min_val=1, max_val=NB * QP)
                v = pe.snap(seen, min_val=1, max_val=NB * QP + NB)
                place = pe.snap(((p - 1) % RQ) * (4 * W), min_val=0, max_val=(RQ - 1) * 4 * W)
                pe.wait_ge(landed, p)
                for h in range(2):
                    pe.wait_ge(oh_ready[h], v)
                    for j in (2 * h, 2 * h + 1):
                        mm = nc.tensor.matmul(AG[b % 2][:, :], onehot[:, j, :], ring[:, ds(place + j * W, W)],
                                              start=False, stop=False, skip_group_check=True)
                        if release and j == 0:
                            mm.then_inc(released, 1)
                    mm.then_inc(oh_used[h], 1)
                pe.reg_add(seen, seen, 1)

            for b in range(NB):
                more = pe.value_load(plan[0:1, 2, b:b + 1], min_val=0, max_val=QP)
                if b >= 2:
                    pe.wait_ge(agg_done, b - 1)
                nc.tensor.matmul(AG[b % 2][:, :], zeros[:, 0:P], zeros[:, :], start=True, stop=False,
                                 skip_group_check=True)
                visit(b, False)
                with pe.If(more > 0):
                    with pe.Fori(0, more):
                        pe.reg_add(pos, pos, 1)
                        visit(b, True)
                nc.tensor.matmul(AG[b % 2][:, 0:2], zeros[:, 0:P], zeros[:, 0:2], start=False, stop=True,
                                 skip_group_check=True).then_inc(agg_full, 1)
                for s, ph in after_block(b):
                    phase(s, ph)

            for i in range(NS):
                pe.wait_ge(diag_ready, 2 + i)
                b = big("wrow", i)
                for j in range(blocks(i)):
                    last = nc.tensor.matmul(b[:, j * P:(j + 1) * P], ones[:, :], diag[:, 4 * i + j, :],
                                            start=True, stop=True)
                last.then_inc(big_full, 1)

        @block.vector
        def _(dve):
            steps = [0]

            def step(ins):
                steps[0] += 1
                ins.then_inc(v_step, 1)
                dve.wait_ge(v_step, steps[0])

            def sm(*key):
                n = at[("sm",) + key]
                dve.wait_ge(sm_full, n + 1)
                return SM[n % 2]

            dve.wait_ge(x_in, 16 * (len(range(0, NB - 1, 8)) + 1))
            for t in range(NB):
                step(nc.vector.bn_stats(st[:, t % 4, :], X[:, t, :]))
                last = nc.vector.bn_aggr(mv[:, t, :], st[:, t % 4, :])
            step(last)
            nc.vector.tensor_scalar(ve[:, :], mv[:, :, 1], EPS, None, ALU.add).then_inc(var_ready, 1)
            dve.wait_ge(std_ready, 1)
            step(nc.vector.reciprocal(rs[:, :], sd[:, :]))
            for s in range(NS):
                for t in range(4 * s, 4 * s + blocks(s)):
                    last = nc.vector.tensor_scalar(Y[:, t, :], X[:, t, :], mv[:, t, 0:1], rs[:, t:t + 1],
                                                   ALU.subtract, ALU.mult)
                last.then_inc(feat_ready, 1)

            dve.wait_ge(consts, N_CONSTS - 1)
            nc.vector.tensor_scalar(ident[:, :], iota[:, :], pcol[:, :], None, ALU.is_equal).then_inc(consts, 1)
            nc.vector.tensor_scalar(before[:, :], iota[:, :], pcol[:, :], None, ALU.is_lt)

            dve.wait_ge(edges_in, 16 * N_EDGE_LOADS)
            nc.vector.tensor_copy(dst_f, dst_i)
            step(nc.vector.scalar_tensor_tensor(row_f, rel_i, float(NB * P), src_i, ALU.mult, ALU.add))
            step(nc.vector.tensor_reduce(tmm[:, 0, :], dst_f.rearrange("p (c e) -> p c e", c=TC), AX.X, ALU.min))
            nc.vector.tensor_reduce(tmm[:, 1, :], dst_f.rearrange("p (c e) -> p c e", c=TC), AX.X,
                                    ALU.max).then_inc(lists_ready, 1)
            dve.wait_ge(lists_ready, 1)
            dve.wait_ge(consts, N_CONSTS)
            for m in range(2):
                for c in range(TC):
                    last = nc.vector.tensor_scalar(diag[:, m * TC + c, :], ident[:, :], tmm[:, m, c:c + 1], None, ALU.mult)
            last.then_inc(diag_ready, 1)

            def lows(s):
                for r in range(2):
                    k = 2 * s + r
                    for j in range(blocks(s)):
                        i = at[("sm", "L2", s, r, j)]
                        dve.wait_ge(hi_ready, sum(1 for x in sm_items[:i + 1] if x[0] == "L2"))
                        nc.vector.scalar_tensor_tensor(stage[:, k % 2, j, D:W], SM[i % 2][:, 0:D], 0.0,
                                                       stage[:, k % 2, j, 0:D], ALU.max,
                                                       ALU.subtract).then_inc(sm_free, 1)

            def make_plan():
                dve.wait_ge(big_free, at[("big", "spread", 3)] + 1)
                step(nc.vector.tensor_scalar(rank[0:32, 0:1], lo_g[:, :], float(P - 1), None, ALU.add))
                step(nc.vector.scalar_tensor_tensor(tmin_b[0:32, :], tmin_b[0:32, :], rank[0:32, 0:1], up[0:32, :],
                                                    ALU.is_le, ALU.mult))
                nc.vector.tensor_reduce(rng[:, 1:2], tmin_b[0:32, :], AX.X, ALU.max)
                step(nc.vector.scalar_tensor_tensor(tmax_b[0:32, :], tmax_b[0:32, :], lo_g[:, :], down[0:32, :],
                                                    ALU.is_ge, ALU.mult))
                step(nc.vector.tensor_reduce(rng[:, 0:1], tmax_b[0:32, :], AX.X, ALU.max))
                nc.vector.tensor_scalar(rng[:, 0:1], rng[:, 0:1], -1.0, float(TW - 1), ALU.mult,
                                        ALU.add).then_inc(range_ready, 1)
                b = sm("ranges")
                step(nc.vector.tensor_copy(q_i[:, :], b[0:1, 0:64]))
                dve.nop().then_inc(sm_free, 1)
                step(nc.vector.tensor_scalar(q_i[:, :], q_i[:, :], 2, None, ALU.arith_shift_right))
                step(nc.vector.tensor_copy(q_f[:, :], q_i[:, :]))
                g = NB
                step(nc.vector.tensor_tensor(okv[:, 0:g - 1], q0[:, 1:g], q1[:, 0:g - 1], ALU.is_ge))
                step(nc.vector.tensor_reduce(okv[:, 31:32], okv[:, 0:g - 1], AX.X, ALU.min))
                nc.vector.memset(pn[:, 0:3, :], 0.0)
                step(nc.vector.memset(pn[:, 3, :], 1.0))
                step(nc.vector.tensor_copy(pn[:, 0, 1:g], q1[:, 0:g - 1]))
                step(nc.vector.tensor_tensor(pn[:, 0, 0:1], q0[:, 0:1], q1[:, 0:1], ALU.min))
                nc.vector.tensor_scalar(pn[:, 1, 0:g], pn[:, 0, 0:g], 1.0, None, ALU.add)
                nc.vector.tensor_copy(pn[:, 3, 1:2], pn[:, 0, 0:1])
                step(nc.vector.tensor_tensor(pn[:, 2, 0:g], q1[:, 0:g], pn[:, 0, 0:g], ALU.subtract))
                step(nc.vector.scalar_tensor_tensor(pn[:, 3, 0:1], q1[:, g - 1:g], 1.0, pn[:, 0, 0:1], ALU.add,
                                                    ALU.subtract))
                step(nc.vector.tensor_tensor(pn[:, :, :], pn[:, :, :], pf[:, :, :], ALU.subtract))
                step(nc.vector.scalar_tensor_tensor(pn[:, :, :], pn[:, :, :], okv[:, 31:32], pf[:, :, :], ALU.mult,
                                                    ALU.add))
                nc.vector.tensor_copy(plan[:, :, :], pn[:, :, :]).then_inc(plan_ready, 1)

            for s in range(NS):
                lows(s)
                if s == 1:
                    make_plan()
            dve.wait_ge(weights_in, 16 * N_LOADS)
            for t in range(NB):
                nc.vector.tensor_tensor(X[:, t, :], X[:, t, :], b3[:, :], ALU.add)
            nc.vector.tensor_tensor(bg[:, :], bi[:, :], bh[:, :], ALU.add).then_inc(bias_ready, 1)

            def norm2(s):
                nb = blocks(s)
                t0 = 4 * s
                for j in range(nb):
                    b = sm("W3", s, j)
                    step(nc.vector.tensor_tensor(X[:, t0 + j, :], X[:, t0 + j, :], b[:, 0:D], ALU.add))
                    dve.sem_inc(sm_free, 1)
                    step(nc.vector.bn_stats(st[:, j, :], X[:, t0 + j, :]))
                    last = nc.vector.bn_aggr(mv[:, t0 + j, :], st[:, j, :])
                step(last)
                nc.vector.tensor_scalar(ve[:, t0:t0 + nb], mv[:, t0:t0 + nb, 1], EPS, None, ALU.add).then_inc(var_ready, 1)
                dve.wait_ge(std_ready, 2 + s)
                step(nc.vector.reciprocal(rs[:, t0:t0 + nb], sd[:, t0:t0 + nb]))
                for j in range(nb):
                    t = t0 + j
                    last = nc.vector.tensor_scalar(n2[:, j, :], X[:, t, :], mv[:, t, 0:1], rs[:, t:t + 1],
                                                   ALU.subtract, ALU.mult)
                last.then_inc(n2_ready, 1)
                dve.wait_ge(n2_ready, s + 1)
                for j in range(nb):
                    t = t0 + j
                    nc.vector.tensor_tensor(X[:, t, :], X[:, t, :], n2[:, j, :], ALU.add)
                    nc.vector.tensor_tensor_reduce(out=junk[:, j * D:(j + 1) * D], in0=n2[:, j, :], in1=wr[:, :], scale=1.0,
                                                   scalar=0.0, op0=ALU.mult, op1=ALU.add,
                                                   accum_out=wcol[:, t:t + 1]).then_inc(v_step, 1)
                steps[0] += nb
                dve.wait_ge(v_step, steps[0])
                step(nc.vector.tensor_scalar(wcol[:, t0:t0 + nb], wcol[:, t0:t0 + nb], br[:, :], None, ALU.add))

            def phase(s, ph):
                n = blocks(s) * P
                if ph == 0:
                    dve.wait_ge(big_free, at[("big", "gate", s, 3)] + 1)
                    nc.vector.tensor_tensor(G[:, 0:2, 0:n], G[:, 0:2, 0:n], G[:, 2:4, 0:n], ALU.mult).then_inc(c_ready, 1)
                    dve.wait_ge(tc_ready, s + 1)
                    nc.vector.tensor_tensor(hnT[:, :, 0:n], G[:, 4:6, 0:n], G[:, 2:4, 0:n], ALU.mult).then_inc(hn_ready, 1)
                elif ph == 1:
                    norm2(s)
                elif ph == 3:
                    for j in range(blocks(s)):
                        b = sm("F2", s, j)
                        nc.vector.tensor_tensor(Y[:, 4 * s + j, :], b[:, 0:D], fb2[:, :], ALU.add).then_inc(sm_free, 1)

            seen = dve.alloc_register("dve_seen")
            dve.reg_mov(seen, 1)
            col = dve.alloc_register("dve_col")

            def visit(b):
                v = dve.snap(seen, min_val=1, max_val=NB * QP + NB)
                c = dve.snap(col, min_val=0, max_val=4 * QP)
                for h in range(2):
                    dve.wait_ge(oh_used[h], v)
                    d = dstT[:, ds(c + 2 * h, 2)].unsqueeze(2).broadcast_to([P, 2, P])
                    nc.vector.scalar_tensor_tensor(onehot[:, 2 * h:2 * h + 2, :], d, float(b * P),
                                                   iota[:, :].unsqueeze(1).broadcast_to([P, 2, P]),
                                                   ALU.subtract, ALU.is_equal).then_inc(oh_ready[h], 1)
                dve.reg_add(seen, seen, 1)

            dve.wait_ge(plan_ready, 1)
            for b in range(NB):
                q = dve.value_load(plan[0:1, 0, b:b + 1], min_val=0, max_val=QP - 1)
                q2 = dve.value_load(plan[0:1, 1, b:b + 1], min_val=0, max_val=QP)
                more = dve.value_load(plan[0:1, 2, b:b + 1], min_val=0, max_val=QP)
                dve.reg_mul(col, q, 4)
                visit(b)
                dve.reg_mul(col, q2, 4)
                with dve.If(more > 0):
                    with dve.Fori(0, more):
                        visit(b)
                        dve.reg_add(col, col, 4)
                dve.wait_ge(agg_copied, b + 1)
                if b % 4 == 0 and b:
                    dve.wait_ge(big_full, at[("big", "aggT", b // 4 - 1, KC - 1)] + 1)
                nc.vector.tensor_tensor(agg[:, b % 4, :], agg_hi[:, :], AG[b % 2][:, D:W], ALU.add).then_inc(agg_done, 1)
                for s, ph in after_block(b):
                    phase(s, ph)

            for i in range(NS):
                for j in range(blocks(i)):
                    t = 4 * i + j
                    last = nc.vector.tensor_scalar(diag[:, t, :], ident[:, :], wcol[:, t:t + 1], None, ALU.mult)
                last.then_inc(diag_ready, 1)
            dve.wait_ge(big_free, at[("big", "wrow", NS - 1)] + 1)
            step(nc.vector.memset(rank4[:, :, :], 0.0))
            for t in range(NB):
                w = wcol[:, t:t + 1]
                a, z = t * P, min(t * P + P, N)

                def count(dst_, lo, hi, op):
                    if hi > lo:
                        step(nc.vector.tensor_scalar(junk[:, lo:hi], w_all[:, lo:hi], w, None, op, ALU.add, accum_out=dst_))
                count(rank4[:, 0, t:t + 1], 0, a, ALU.is_ge)
                count(rank4[:, 1, t:t + 1], a, N, ALU.is_gt)
                step(nc.vector.scalar_tensor_tensor(junk[:, a:z], w_all[:, a:z], w, before[:, 0:z - a], ALU.is_equal,
                                                    ALU.mult, accum_out=rank4[:, 2, t:t + 1]))
            step(nc.vector.tensor_tensor(rank[:, :], rank4[:, 0, :], rank4[:, 1, :], ALU.add))
            step(nc.vector.tensor_tensor(rank[:, :], rank[:, :], rank4[:, 2, :], ALU.add))
            step(nc.vector.scalar_tensor_tensor(mw[:, :], rank[:, :], float(NSEL), wcol[:, :], ALU.is_lt, ALU.mult))
            for t in range(NB):
                nc.vector.scalar_tensor_tensor(X[:, t, :], Y[:, t, :], mw[:, t:t + 1], X[:, t, :], ALU.mult,
                                               ALU.add).then_inc(out_ready, 1)


N_LOADS = 18
N_EDGE_LOADS = 9
N_CONSTS = 17


def kernel(**inputs):
    import numpy as np
    import concourse.bacc as bacc
    from concourse.bass_utils import run_bass_kernel_spmd

    a = {k: np.asarray(v) for k, v in inputs.items()}
    D = a["x"].shape[1]

    def gates(w):
        return np.concatenate([w[0:D], w[2 * D:3 * D], w[3 * D:4 * D]])

    def cols(v):
        return v.reshape(-1, P).T

    laid = {
        "x": a["x"], "src": a["src"], "dst": a["dst"], "rel": a["edge_type_2"],
        "w_rel_t": a["L0_gnn_W_rel"].transpose(0, 2, 1),
        "b_rel_col": cols(a["L0_gnn_b_rel"]), "b_rel_row": a["L0_gnn_b_rel"].reshape(1, -1),
        "w_ih_t": gates(a["L0_gnn_W_ih"]).T, "b_ih_col": cols(gates(a["L0_gnn_b_ih"])),
        "b_hh_col": cols(gates(a["L0_gnn_b_hh"])),
        "w1_t": a["L0_gnn_W1"].T, "b1_col": cols(a["L0_gnn_b1"]),
        "w2_t": a["L0_gnn_W2"].T, "b2_col": cols(a["L0_gnn_b2"]),
        "w3_t": a["L0_gnn_W3"].T, "b3_row": a["L0_gnn_b3"].reshape(1, -1),
        "wr_row": a["L0_ffn_wr"].reshape(1, -1), "br_one": a["L0_ffn_br"].reshape(1, 1),
        "f1": a["L0_ffn_w1"], "f1_col": cols(a["L0_ffn_b1"]), "f2": a["L0_ffn_w2"],
        "f2_row": a["L0_ffn_b2"].reshape(1, -1),
    }
    nc = bacc.Bacc("TRN2", target_bir_lowering=False, num_devices=1)
    arrays, args = {}, []
    for name, v in laid.items():
        v = np.ascontiguousarray(v)
        arrays[f"in_{name}"] = v
        args.append(nc.dram_tensor(f"in_{name}", v.shape, mybir.dt.from_np(v.dtype), kind="ExternalInput").ap())
    args.append(nc.dram_tensor("out", a["x"].shape, F32, kind="ExternalOutput").ap())
    build(nc, *args)
    r = run_bass_kernel_spmd(nc, [arrays], core_ids=[0])
    return r.results[0]["out"]
```

```python
from contextlib import ExitStack

import concourse.bass as bass
from concourse import mybir

ALU = mybir.AluOpType
ACT = mybir.ActivationFunctionType
AX = mybir.AxisListType
F32 = mybir.dt.float32
F16 = mybir.dt.float16
I32 = mybir.dt.int32
ds = bass.ds

P = 128
EPS = 1e-5
PAD_DST = 30000


def build(nc, x, src, dst, rel, w_rel_t, b_rel_col, b_rel_row, w_ih_t, b_ih_col, b_hh_col, w1_t, b1_col, w2_t, b2_col,
          w3_t, b3_row, wr_row, br_one, f1, f1_col, f2, f2_row, out):
    N, D = x.shape
    E = src.shape[0]
    H = f1.shape[1]
    KC = D // P
    HC = H // P
    NB = -(-N // P)
    NS = -(-NB // 4)
    LAST = N - (NB - 1) * P
    TE = -(-E // P)
    TC = -(-(TE + 4) // P)
    TW = TC * P
    RQ = 8
    QP = -(-(-(-TE // 4) + 1) // RQ) * RQ
    NSEL = max(1, int(0.5 * N)) - 1
    W = 2 * D
    HOT = 1
    A = 2 * NB
    PARTS = 2
    SLACK = 20.0
    GAP = 10.0
    GN = 512 // A
    GC = GN * A
    HG = -(-HOT * P // GN)
    CN = HG * GN
    MK = 4
    ML = -(-A // MK)
    CENTER = NB * P // 2
    OR = 4
    SCALE = 64.0
    MAX_TILES = 2048 // P
    AB = 8
    assert D == 256 and CENTER <= 2048 and NB * P < PAD_DST and 3 * TW <= NB * P and (QP + RQ) * 4 <= TW

    def blocks(s):
        return min(4, NB - 4 * s)

    with ExitStack() as ctx:
        def sb(name, shape, dt=F32):
            return ctx.enter_context(nc.sbuf_tensor(name, shape, dt))

        def sem(name):
            return ctx.enter_context(nc.semaphore(name))

        table = nc.dram_tensor("message_table", [2 * NB * P, W], F16).ap()

        X = sb("X", [P, NB, D])
        late = sb("late", [P, NB * D + 6 * 512 + HC * 512])
        Y = late[:, 0:NB * D].rearrange("p (t d) -> p t d", d=D)
        G = late[:, NB * D:NB * D + 6 * 512].rearrange("p (g n) -> p g n", g=6)
        big = late[:, NB * D + 6 * 512:NB * D + (6 + HC) * 512]
        counts = late[:, NB * D:].bitcast(F16)[:, 0:A * CN].rearrange("p (a n) -> p a n", a=A)
        ring = sb("ring", [P, RQ * 4 * W], F16)
        prep = ring[:, :].bitcast(F32)
        raw_i = ring[:, :].bitcast(I32)

        def pv(n, v=prep):
            return v[:, n * TW:(n + 1) * TW]
        prep_g = late[:, NB * D:NB * D + 6 * 512]
        src_i, dst_i, rel_i = pv(0, raw_i), pv(1, raw_i), pv(2, raw_i)
        dst_f, row_f = pv(3), pv(4)
        tmin_b, tmax_b = pv(5), pv(0, prep_g)
        up, down = pv(1, prep_g), pv(2, prep_g)
        tmp, keys_i, keys_i2 = dst_f, src_i, rel_i
        dst16 = sb("dst16", [P, TW], F16)
        iota_b = sb("iota_b", [P, 2, P], F16)
        rowT = sb("rowT", [P, TW], I32)
        rows4 = sb("rows4", [P, RQ * 4], I32)
        onehot = sb("onehot", [P, OR * 4 * P], F16)
        hT = big[:, :].rearrange("p (c n) -> p c n", c=HC)
        h1T = big[:, 0:2048].rearrange("p (r c n) -> p r c n", r=2, c=KC)
        stage = big[:, 2048:4096].bitcast(F16).rearrange("p (b t w) -> p b t w", b=2, t=4)
        assert HOT == 1 and A * CN // 2 + MK * W <= 6 * 512 + HC * 512 and MK * W == 2048
        mring = big[:, 2048:4096].bitcast(F16).rearrange("p (b a w) -> p b a w", b=2, a=MK)
        diag_lists = prep[:, 6 * TW:8 * TW].rearrange("p (c n) -> p c n", n=P)
        w_all = sb("w_all", [P, NB * P])
        dstT = w_all[:, 2 * TW:3 * TW]
        oh_hot = sb("oh_hot", [P, 4 * (P + GC)], F16)
        oh_row = oh_hot[:, 0:4 * P].rearrange("p (t n) -> p t n", t=4)
        oh_key = oh_hot[:, 4 * P:].rearrange("p (t n) -> p t n", t=4)
        junk = oh_hot.bitcast(mybir.dt.bfloat16)
        iota16 = sb("iota16", [P, 512], F16)
        kb = w_all[:, 0:2 * TW].rearrange("p (t k) -> p t k", k=2)
        kb4 = sb("kb4", [P, 4, 2])
        fT = sb("fT", [P, KC, 512])
        aggT = sb("aggT", [P, KC, 512])
        hnT = G[:, 0:2, :]
        n2 = sb("n2", [P, 4, D])
        agg = sb("agg", [P, AB, D])
        agg_hi = sb("agg_hi", [P, D])
        diag = sb("diag", [P, 4, P])
        WR = sb("WR", [P, 2, KC, D])
        WI = sb("WI", [P, KC, 3 * D])
        W1 = sb("W1", [P, KC, P])
        W2 = sb("W2", [P, P])
        W3 = sb("W3", [P, D])
        F1 = sb("F1", [P, KC, H])
        F2 = sb("F2", [P, HC, D])
        br_col = sb("br_col", [P, 4])
        br_row = sb("br_row", [1, 2 * D])
        bi = sb("bi", [P, 6])
        bh = sb("bh", [P, 6])
        bg = sb("bg", [P, 6])
        b1 = sb("b1", [P, 1])
        b2 = sb("b2", [P, 1])
        b3 = sb("b3", [P, D])
        wr = sb("wr", [P, D])
        br = sb("br", [P, 1])
        fb1 = sb("fb1", [P, HC])
        fb2 = sb("fb2", [P, D])
        ident = sb("ident", [P, P])
        ones = sb("ones", [P, P])
        zeros = sb("zeros", [P, 512], F16)
        iota = sb("iota", [P, P])
        pcol = sb("pcol", [P, 1])
        before = sb("before", [P, P])
        lo_g = sb("lo_g", [P, 2])
        nodes = sb("nodes", [P, HOT])
        tiles_of = sb("tiles_of", [P, HOT])
        st = sb("st", [P, 4, 6])
        mv = sb("mv", [P, NB, 2])
        ve = sb("ve", [P, NB])
        sd = sb("sd", [P, NB])
        rs = sb("rs", [P, NB])
        wcol = sb("wcol", [P, NB])
        tmm = sb("tmm", [P, 2, TC])
        rng = sb("rng", [P, 3])
        q_i = sb("q_i", [1, 2 * P], I32)
        q_f = sb("q_f", [1, 2 * P])
        q0, q1 = q_f[:, 64:128], q_f[:, P + 64:2 * P]
        h0, h1 = q_f[:, 0:64], q_f[:, P:P + 64]
        okv = sb("okv", [1, 40])
        pn = sb("pn", [1, 6, 64])
        pf = sb("pf", [1, 6, 64])
        plan = sb("plan", [1, 8, 64], I32)
        rank4 = sb("rank4", [P, NB, 4 + NS])
        rank = sb("rank", [P, NB])
        mw = sb("mw", [P, NB])

        AG = [ctx.enter_context(nc.psum_tensor(f"AG{i}", [P, 512], F32)) for i in range(2)]
        BIG = [ctx.enter_context(nc.psum_tensor(f"BIG{i}", [P, 512], F32)) for i in range(4)]
        SM = [ctx.enter_context(nc.psum_tensor(f"SM{i}", [P, 512], F32)) for i in range(2)]

        x_in = sem("x_in")
        edges_in = sem("edges_in")
        pads_set = sem("pads_set")
        weights_in = sem("weights_in")
        bias_ready = sem("bias_ready")
        scaled = sem("scaled")
        consts = sem("consts")
        v_step = sem("v_step")
        feat_ready = sem("feat_ready")
        var_ready = sem("var_ready")
        std_ready = sem("std_ready")
        big_full = sem("big_full")
        big_free = sem("big_free")
        sm_full = sem("sm_full")
        sm_free = sem("sm_free")
        hi_ready = sem("hi_ready")
        stored = [sem(f"stored{i}") for i in range(2)]
        lists_ready = sem("lists_ready")
        hot_ready = [sem(f"hot_ready{i}") for i in range(2)]
        hot_used = [sem(f"hot_used{i}") for i in range(2)]
        kb_ready = sem("kb_ready")
        m_in = [sem(f"m_in{i}") for i in range(2)]
        m_used = sem("m_used")
        hot_added = sem("hot_added")
        keys_ready = sem("keys_ready")
        diag_ready = sem("diag_ready")
        range_ready = sem("range_ready")
        plan_ready = sem("plan_ready")
        idx_ready = sem("idx_ready")
        idx_seen = sem("idx_seen")
        gathered = [sem(f"gathered{i}") for i in range(RQ)]
        landed = sem("landed")
        released = sem("released")
        oh_ready = sem("oh_ready")
        oh_used = sem("oh_used")
        agg_full = sem("agg_full")
        agg_copied = sem("agg_copied")
        agg_done = sem("agg_done")
        c_ready = sem("c_ready")
        tc_ready = sem("tc_ready")
        hn_ready = sem("hn_ready")
        n2_ready = sem("n2_ready")
        nodes_ready = sem("nodes_ready")
        out_ready = sem("out_ready")
        out_done = sem("out_done")

        big_items, sm_items, at = [], [], {}

        def note(kind, key):
            lst = big_items if kind == "big" else sm_items
            at[(kind,) + key] = len(lst)
            lst.append(key)

        steps_of = []

        def tallies(s):
            old, step = 4 * s, 4 if s < NS - 1 else 4 * NS
            first = [((s, t, min(t + step, old)), 0.8 * step) for t in range(0, old, step)]
            return first + [((s, t, t + 1), 1.0 + 0.14 * t) for t in range(old, old + blocks(s))]

        def schedule():
            quad = 4.4

            def quads_before(node):
                return TE / 4 * (min(node, N) / N) ** 0.5

            fill = [([("counts", g)], 3 + 2.2 * (1 + quads_before(GN * g + GN) - quads_before(GN * g))) for g in range(HG)]
            fill += [([("dense", k)], 2.0) for k in range(ML)]
            left = []
            for s in range(NS + 1):
                w = blocks(s) / 4 if s < NS else 0
                v = blocks(s - 1) / 4 if s else 0
                for n, (ph, k, c) in enumerate((("gates", s, 14 * w), ("down0", s - 1, 7 * v), ("mlp", s, 11 * w),
                                                ("down1", s - 1, 7 * v), ("hidden0", s, 9 * w), ("rank", s, 2 * w),
                                                ("hidden1", s, 8 * w))):
                    if ph == "hidden1" and k < NS:
                        left = tallies(k)
                        share = sum(x[1] for x in left) / 6
                    now = []
                    spent = 0.0
                    while left and ph != "rank" and spent + left[0][1] / 2 < share:
                        spent += left[0][1]
                        now.append(("tally", left.pop(0)[0]))
                    if ph == "hidden0":
                        now += [("tally", x[0]) for x in left]
                        left = []
                    if 0 <= k < NS:
                        now.append((ph, k))
                    if now:
                        fill.append((now, c))
            now = 0.0
            landed_at, seen_at = [], []
            for b in range(NB):
                ends = [round(quads_before(max(b + k / PARTS, HOT) * P) - quads_before(HOT * P)) for k in range(PARTS + 1)]
                for part in range(PARTS):
                    while len(landed_at) <= ends[part]:
                        q = len(landed_at)
                        landed_at.append(max([landed_at[-1] if q else 0.0] + seen_at[q - RQ:q - RQ + 1] * (q >= RQ)) + quad)
                    spent = 0.0
                    while fill and b >= HOT:
                        bundle, c = fill[0]
                        must = part == 0 and b >= AB and any(("gates", (b - AB) // 4) in x[0] for x in fill)
                        ready = all(kind in ("counts", "dense", "tally") or 4 * s + blocks(s) <= b for kind, s in bundle)
                        if not must and (not ready or now + min(c, 10.0) > landed_at[ends[part]] + SLACK
                                         or b >= AB and spent + c / 2 > GAP):
                            break
                        steps_of.extend(fill.pop(0)[0])
                        now += c
                        spent += c
                    steps_of.append(("visit" if part == 0 else "more", b))
                    now += 1.0
                    while len(seen_at) < ends[part + 1]:
                        q = len(seen_at)
                        if len(landed_at) <= q:
                            landed_at.append(max([landed_at[-1]] + seen_at[q - RQ:q - RQ + 1] * (q >= RQ)) + quad)
                        now = max(now, landed_at[q]) + 0.9
                        seen_at.append(now)
            for x in fill:
                steps_of.extend(x[0])

        def order():
            def turn(s):
                for c in range(KC):
                    note("big", ("featT", s, c))
            turn(0)
            for s in range(NS):
                for r in range(2):
                    for m in range(KC):
                        note("big", ("L1", s, r, m))
                if s + 1 < NS:
                    turn(s + 1)
                for r in range(2):
                    for j in range(blocks(s)):
                        note("sm", ("L2", s, r, j))
                if s == 1:
                    for n in range(4):
                        note("big", ("lists", n))
                    for n in range(4):
                        note("big", ("spread", n))
                    note("sm", ("ranges",))
            for kind, s in steps_of:
                if kind == "counts":
                    note("big", ("counts", s))
                elif kind == "dense" and s == 0:
                    for c in range(KC):
                        note("big", ("hotT", c))
                elif kind == "gates":
                    for c in range(KC):
                        note("big", ("aggT", s, c))
                    for g in range(6):
                        note("big", ("gate", s, g))
                elif kind == "mlp":
                    note("big", ("W1", s))
                    note("big", ("W2", s))
                    for j in range(blocks(s)):
                        note("sm", ("W3", s, j))
                elif kind in ("hidden0", "hidden1"):
                    if kind == "hidden0":
                        for c in range(KC):
                            note("big", ("n2T", s, c))
                    for c in chunks(kind):
                        note("big", ("F1", s, c))
                elif kind == "rank":
                    note("big", ("wrow", s))
                elif kind in ("down0", "down1"):
                    for j in pieces(kind, s):
                        note("sm", ("F2", s, j))

        def chunks(kind):
            return range(0, HC // 2) if kind == "hidden0" else range(HC // 2, HC)

        def pieces(kind, s):
            h = -(-blocks(s) // 2)
            return range(0, h) if kind == "down0" else range(h, blocks(s))

        schedule()
        order()

        block = ctx.enter_context(nc.Block())

        @block.sync
        def _(sp):
            for n in range(0, NB - 1, 8):
                sp.dma_start(X[:, n:n + 8, :], x[n * P:(n + 8) * P, :].rearrange("(t p) d -> p t d", p=P)).then_inc(x_in, 16)
            sp.wait_ge(pads_set, 1)
            sp.dma_start(X[0:LAST, NB - 1, :], x[(NB - 1) * P:N, :]).then_inc(x_in, 16)
            full = E // P
            wide = full // P
            sp.wait_ge(pads_set, 4)
            for a, t in ((src, src_i), (dst, dst_i), (rel, rel_i)):
                t3 = t.rearrange("p (c e) -> p c e", c=TC)
                sp.dma_start(t3[:, 0:wide, :], a[0:wide * P * P].rearrange("(c p e) -> p c e", p=P, e=P)).then_inc(edges_in, 16)
                if full > wide * P:
                    sp.dma_start(t3[0:full - wide * P, wide, :],
                                 a[wide * P * P:full * P].rearrange("(p e) -> p e", e=P)).then_inc(edges_in, 16)
                if E > full * P:
                    sp.dma_start(t3[full - wide * P:full - wide * P + 1, wide, 0:E - full * P],
                                 a[full * P:E].rearrange("(p e) -> p e", p=1)).then_inc(edges_in, 16)
            for s in range(NS):
                n = blocks(s)
                for r in range(2):
                    k = 2 * s + r
                    sp.wait_ge(sm_free, at[("sm", "L2", s, r, n - 1)] + 1)
                    row = (r * NB + 4 * s) * P
                    sp.dma_start(table[row:row + n * P, :].rearrange("(t p) w -> p t w", p=P),
                                 stage[:, k % 2, 0:n, :]).then_inc(stored[k % 2], 16)
            sp.wait_ge(plan_ready, 1)
            quads = sp.value_load(plan[0:1, 3, 0:1], min_val=1, max_val=QP)
            passes = sp.value_load(plan[0:1, 3, 2:3], min_val=1, max_val=NB)
            want = sp.alloc_register("want")
            sp.reg_mov(want, 64)
            with sp.Fori(0, passes):
                with sp.Fori(0, quads, RQ):
                    w = sp.snap(want)
                    for j in range(RQ):
                        sp.wait_ge(gathered[j], w)
                        sp.sem_inc(landed, 1)
                    sp.reg_add(want, want, 64)
            for n in range(NB):
                sp.wait_ge(out_ready, n + 1)
                if n < NB - 1:
                    sp.dma_start(out[n * P:(n + 1) * P, :], X[:, n, :]).then_inc(out_done, 16)
                else:
                    sp.dma_start(out[n * P:N, :], X[0:LAST, n, :]).then_inc(out_done, 16)
            sp.wait_ge(out_done, 16 * NB)

        @block.gpsimd
        def _(pool):
            nc.gpsimd.memset(X[:, NB - 1, :], 0.0).then_inc(pads_set, 1)
            nc.gpsimd.memset(src_i, 0).then_inc(pads_set, 1)
            nc.gpsimd.memset(rel_i, 0).then_inc(pads_set, 1)
            nc.gpsimd.memset(dst_i, PAD_DST).then_inc(pads_set, 1)
            nc.gpsimd.iota(iota[:, :], pattern=[[1, P]], base=0, channel_multiplier=0,
                           allow_small_or_imprecise_dtypes=True).then_inc(consts, 1)
            nc.gpsimd.iota(pcol[:, :], pattern=[[1, 1]], base=0, channel_multiplier=1,
                           allow_small_or_imprecise_dtypes=True).then_inc(consts, 1)
            nc.gpsimd.memset(ones[:, :], 1.0).then_inc(consts, 1)
            nc.gpsimd.memset(zeros[:, :], 0.0).then_inc(consts, 1)
            nc.gpsimd.iota(up, pattern=[[1, TW]], base=0, channel_multiplier=0,
                           allow_small_or_imprecise_dtypes=True).then_inc(consts, 1)
            nc.gpsimd.iota(down, pattern=[[-1, TW]], base=TW - 1, channel_multiplier=0,
                           allow_small_or_imprecise_dtypes=True).then_inc(consts, 1)
            for k, (lo, n) in enumerate(((0, GN), (64, P))):
                pool.wait_ge(consts, 6 + 2 * k)
                nc.gpsimd.iota(lo_g[lo:lo + 64, 0:1], pattern=[[1, 1]], base=0, channel_multiplier=n,
                               allow_small_or_imprecise_dtypes=True).then_inc(consts, 1)
                nc.gpsimd.iota(lo_g[lo:lo + 64, 1:2], pattern=[[1, 1]], base=n - 1, channel_multiplier=n,
                               allow_small_or_imprecise_dtypes=True).then_inc(consts, 1)
            pool.wait_ge(consts, 10)
            nc.gpsimd.iota(nodes[:, :], pattern=[[P, HOT]], base=0, channel_multiplier=1,
                           allow_small_or_imprecise_dtypes=True).then_inc(consts, 1)
            nc.gpsimd.iota(iota16[:, :], pattern=[[1, 512]], base=0, channel_multiplier=0,
                           allow_small_or_imprecise_dtypes=True).then_inc(consts, 1)
            for row, v in enumerate((QP - 1, 0, QP, NB, QP - 1, 1)):
                nc.gpsimd.memset(pf[:, row, :], float(v)).then_inc(consts, 1)
            pool.wait_ge(consts, 18)
            nc.gpsimd.memset(pf[:, 0, 0:1], 0.0).then_inc(consts, 1)
            nc.gpsimd.memset(pf[:, 1, 0:1], 1.0).then_inc(consts, 1)
            nc.gpsimd.memset(pf[:, 2, 0:1], float(QP - 1)).then_inc(consts, 1)
            nc.gpsimd.memset(pf[:, 3, 0:1], float(QP)).then_inc(consts, 1)
            nc.gpsimd.memset(pf[:, 3, 1:2], 0.0).then_inc(consts, 1)

            pool.wait_ge(plan_ready, 1)
            quads = pool.value_load(plan[0:1, 3, 0:1], min_val=1, max_val=QP)
            first = pool.value_load(plan[0:1, 3, 1:2], min_val=0, max_val=QP - 1)
            passes = pool.value_load(plan[0:1, 3, 2:3], min_val=1, max_val=NB)
            for k in range(2):
                pool.wait_ge(stored[k], 16 * NS)
            pos = pool.alloc_register("pos")
            col = pool.alloc_register("col")
            pool.reg_mov(pos, 0)
            with pool.Fori(0, passes):
                pool.reg_mul(col, first, 4)
                with pool.Fori(0, quads, RQ):
                    p0 = pool.snap(pos, min_val=0, max_val=NB * QP)
                    c0 = pool.snap(col, min_val=0, max_val=QP * 4)
                    for j in range(RQ):
                        pool.wait_ge(released, p0 + (j + 1))
                        nc.gpsimd.tensor_copy(rows4[:, 4 * j:4 * j + 4], rowT[:, ds(c0 + 4 * j, 4)]).then_inc(idx_ready, 1)
                        pool.wait_ge(idx_ready, p0 + (j + 1))
                        pool.sem_inc(idx_seen, 1)
                        for i in range(4):
                            k = 4 * j + i
                            nc.gpsimd.indirect_dma_start(
                                ring[:, k * W:(k + 1) * W], None, table,
                                bass.IndirectOffsetOnAxis(ap=rows4[:, k:k + 1], axis=0)).then_inc(gathered[j], 16)
                    pool.reg_add(pos, pos, RQ)
                    pool.reg_add(col, col, 4 * RQ)

        @block.scalar
        def _(act):
            loads = [(WR[:, :, :, :], w_rel_t.rearrange("r (c p) n -> p r c n", p=P)),
                     (br_col[:, :], b_rel_col), (br_row[:, :], b_rel_row),
                     (WI[:, :, :], w_ih_t.rearrange("(c p) n -> p c n", p=P)),
                     (bi[:, :], b_ih_col), (bh[:, :], b_hh_col),
                     (W1[:, :, :], w1_t.rearrange("(c p) n -> p c n", p=P)), (b1[:, :], b1_col),
                     (W2[:, :], w2_t), (b2[:, :], b2_col), (W3[:, :], w3_t),
                     (b3[:, :], b3_row.broadcast_to([P, D])), (wr[:, :], wr_row.broadcast_to([P, D])),
                     (br[:, :], br_one.broadcast_to([P, 1])),
                     (F1[:, :, :], f1.rearrange("(c p) n -> p c n", p=P)), (fb1[:, :], f1_col),
                     (F2[:, :, :], f2.rearrange("(c p) n -> p c n", p=P)), (fb2[:, :], f2_row.broadcast_to([P, D]))]
            assert len(loads) == N_LOADS
            for t, a in loads:
                act.dma_start(t, a).then_inc(weights_in, 16)

            def big(*key):
                n = at[("big",) + key]
                act.wait_ge(big_full, n + 1)
                return BIG[n % 4]

            def roots(n, lo, hi):
                act.wait_ge(var_ready, n)
                nc.scalar.activation(sd[:, lo:hi], ve[:, lo:hi], ACT.Sqrt).then_inc(std_ready, 1)

            def turn(s):
                for c in range(KC):
                    b = big("featT", s, c)
                    n = blocks(s) * P
                    nc.scalar.activation(fT[:, c, 0:n], b[:, 0:n], ACT.Copy).then_inc(big_free, 1)

            roots(1, 0, 4)
            turn(0)
            roots(2, 4, NB)
            act.wait_ge(weights_in, 16 * N_LOADS)
            act.wait_ge(scaled, 1)
            for s in range(NS):
                n = blocks(s) * P
                for r in range(2):
                    for m in range(KC):
                        b = big("L1", s, r, m)
                        nc.scalar.activation(h1T[:, r, m, 0:n], b[:, 0:n], ACT.Relu,
                                             bias=br_col[:, 2 * r + m:2 * r + m + 1],
                                             scale=SCALE).then_inc(big_free, 1)
                if s + 1 < NS:
                    turn(s + 1)
                for r in range(2):
                    k = 2 * s + r
                    if k >= 2:
                        act.wait_ge(stored[k % 2], 16 * (k // 2))
                    for j in range(blocks(s)):
                        i = at[("sm", "L2", s, r, j)]
                        act.wait_ge(sm_full, i + 1)
                        nc.scalar.activation(stage[:, k % 2, j, 0:D], SM[i % 2][:, 0:D], ACT.Relu).then_inc(hi_ready, 1)
                if s == 1:
                    for i in range(4):
                        b = big("lists", i)
                        w = min(4, TC - 4 * (i % 2)) * P
                        o = (i % 2) * 4 * P
                        nc.scalar.activation((dstT if i < 2 else rowT)[:, o:o + w], b[:, 0:w], ACT.Copy).then_inc(big_free, 1)
                    for i in range(4):
                        b = big("spread", i)
                        w = min(4, TC - 4 * (i % 2)) * P
                        o = (i % 2) * 4 * P
                        nc.scalar.activation((tmin_b if i < 2 else tmax_b)[:, o:o + w], b[:, 0:w],
                                             ACT.Copy).then_inc(big_free, 1)

            def load_table(k):
                if k < ML:
                    if k >= 2:
                        act.wait_ge(m_used, k - 1)
                    n = min(MK, A - k * MK)
                    act.dma_start(mring[:, k % 2, 0:n, :],
                                  table[k * MK * P:(k * MK + n) * P, :].rearrange("(a p) w -> p a w", p=P)).then_inc(m_in[k % 2], 16)

            for k in range(2):
                act.wait_ge(stored[k], 16 * NS)
            load_table(0)
            load_table(1)
            act.wait_ge(bias_ready, 1)
            for kind, s in steps_of:
                n = 0 if kind in ("visit", "more", "counts", "dense", "tally") else blocks(s) * P
                if kind == "more":
                    act.wait_ge(agg_full, s + 1)
                    if s:
                        act.wait_ge(agg_done, s)
                    nc.scalar.activation(agg_hi[:, :], AG[s % 2][:, 0:D], ACT.Copy, scale=1 / SCALE).then_inc(agg_copied, 1)
                elif kind == "counts":
                    b = big("counts", s)
                    nc.scalar.activation(counts[:, :, s * GN:(s + 1) * GN].rearrange("p a n -> p n a"),
                                         b[:, 0:GC].rearrange("p (n a) -> p n a", a=A), ACT.Copy).then_inc(big_free, 1)
                elif kind == "dense":
                    load_table(s + 2)
                    if s == ML - 1:
                        for c in range(KC):
                            b = big("hotT", c)
                            nc.scalar.activation(fT[:, c, 0:HOT * P], b[:, 0:HOT * P], ACT.Copy, scale=1 / SCALE).then_inc(big_free, 1)
                elif kind == "gates":
                    for c in range(KC):
                        b = big("aggT", s, c)
                        nc.scalar.activation(aggT[:, c, 0:n], b[:, 0:n], ACT.Copy).then_inc(big_free, 1)
                    for g in range(6):
                        b = big("gate", s, g)
                        nc.scalar.activation(G[:, g, 0:n], b[:, 0:n], ACT.Tanh if g in (2, 3) else ACT.Sigmoid,
                                             bias=bg[:, g:g + 1]).then_inc(big_free, 1)
                    act.wait_ge(c_ready, s + 1)
                    nc.scalar.activation(G[:, 2:4, 0:n], G[:, 0:2, 0:n], ACT.Tanh).then_inc(tc_ready, 1)
                elif kind == "mlp":
                    b = big("W1", s)
                    nc.scalar.activation(aggT[:, 0, 0:n], b[:, 0:n], ACT.Relu, bias=b1[:, :]).then_inc(big_free, 1)
                    b = big("W2", s)
                    nc.scalar.activation(aggT[:, 1, 0:n], b[:, 0:n], ACT.Relu, bias=b2[:, :]).then_inc(big_free, 1)
                    roots(3 + s, 4 * s, 4 * s + blocks(s))
                elif kind in ("hidden0", "hidden1"):
                    if kind == "hidden0":
                        for c in range(KC):
                            b = big("n2T", s, c)
                            nc.scalar.activation(fT[:, c, 0:n], b[:, 0:n], ACT.Copy).then_inc(big_free, 1)
                    for c in chunks(kind):
                        b = big("F1", s, c)
                        nc.scalar.activation(hT[:, c, 0:n], b[:, 0:n], ACT.Gelu_apprx_tanh,
                                             bias=fb1[:, c:c + 1]).then_inc(big_free, 1)
                elif kind == "rank":
                    b = big("wrow", s)
                    nc.scalar.activation(w_all[:, 4 * s * P:4 * s * P + n], b[:, 0:n], ACT.Copy).then_inc(big_free, 1)

        @block.tensor
        def _(pe):
            def big(*key):
                n = at[("big",) + key]
                if n >= 4:
                    pe.wait_ge(big_free, n - 3)
                return BIG[n % 4]

            def sm(*key):
                n = at[("sm",) + key]
                if n >= 2:
                    pe.wait_ge(sm_free, n - 1)
                return SM[n % 2]

            def read(*key):
                pe.wait_ge(big_free, at[("big",) + key] + 1)

            def turn(name, s, tile):
                for c in range(KC):
                    b = big(name, s, c)
                    for j in range(blocks(s)):
                        last = nc.tensor.transpose(b[:, j * P:(j + 1) * P], tile(j)[:, c * P:(c + 1) * P], ident[:, :])
                    last.then_inc(big_full, 1)

            def feat(s):
                if s == 0:
                    pe.wait_ge(consts, N_CONSTS)
                pe.wait_ge(feat_ready, s + 1)
                turn("featT", s, lambda j: Y[:, 4 * s + j, :])

            feat(0)
            pe.wait_ge(weights_in, 16 * N_LOADS)
            pe.wait_ge(scaled, 1)
            for s in range(NS):
                n = blocks(s) * P
                read("featT", s, KC - 1)
                for r in range(2):
                    for m in range(KC):
                        b = big("L1", s, r, m)
                        for k in range(KC):
                            last = nc.tensor.matmul(b[:, 0:n], WR[:, r, k, m * P:(m + 1) * P], fT[:, k, 0:n],
                                                    start=(k == 0), stop=(k == KC - 1))
                        last.then_inc(big_full, 1)
                if s + 1 < NS:
                    feat(s + 1)
                for r in range(2):
                    read("L1", s, r, KC - 1)
                    for j in range(blocks(s)):
                        b = sm("L2", s, r, j)
                        for k in range(KC):
                            nc.tensor.matmul(b[:, 0:D], h1T[:, r, k, j * P:(j + 1) * P], WR[:, r, k, :],
                                             start=(k == 0), stop=False)
                        nc.tensor.matmul(b[:, 0:D], ones[0:1, :], br_row[:, r * D:(r + 1) * D],
                                         start=False, stop=True).then_inc(sm_full, 1)
                if s == 1:
                    pe.wait_ge(lists_ready, 1)
                    for i in range(4):
                        b = big("lists", i)
                        for c in range(4 * (i % 2), min(4 * (i % 2) + 4, TC)):
                            last = nc.tensor.transpose(b[:, (c % 4) * P:(c % 4 + 1) * P],
                                                       (dst_f if i < 2 else row_f)[:, c * P:(c + 1) * P], ident[:, :])
                        last.then_inc(big_full, 1)
                    pe.wait_ge(diag_ready, 1)
                    for i in range(4):
                        b = big("spread", i)
                        for c in range(4 * (i % 2), min(4 * (i % 2) + 4, TC)):
                            last = nc.tensor.matmul(b[:, (c % 4) * P:(c % 4 + 1) * P], ones[:, :],
                                                    diag_lists[:, (i // 2) * TC + c, :], start=True, stop=True)
                        last.then_inc(big_full, 1)
                    pe.wait_ge(range_ready, 1)
                    b = sm("ranges")
                    nc.tensor.transpose(b[0:1, 0:P], rng[:, 0:1], ident[:, :])
                    nc.tensor.transpose(b[0:1, P:2 * P], rng[:, 1:2], ident[:, :])
                    nc.tensor.transpose(b[0:1, 2 * P:3 * P], rng[:, 2:3], ident[:, :]).then_inc(sm_full, 1)

            def phase(kind, s):
                nb = blocks(s)
                n = nb * P
                if kind == "gates":
                    pe.wait_ge(agg_done, 4 * s + nb)
                    turn("aggT", s, lambda j: agg[:, (4 * s + j) % AB, :])
                    if s == 0:
                        pe.wait_ge(hot_added, 1)
                    else:
                        read("aggT", s, KC - 1)
                    for g in range(6):
                        b = big("gate", s, g)
                        for k in range(KC):
                            last = nc.tensor.matmul(b[:, 0:n], WI[:, k, g * P:(g + 1) * P], aggT[:, k, 0:n],
                                                    start=(k == 0), stop=(k == KC - 1))
                        last.then_inc(big_full, 1)
                elif kind == "mlp":
                    pe.wait_ge(hn_ready, s + 1)
                    b = big("W1", s)
                    for k in range(KC):
                        last = nc.tensor.matmul(b[:, 0:n], W1[:, k, :], hnT[:, k, 0:n], start=(k == 0), stop=(k == KC - 1))
                    last.then_inc(big_full, 1)
                    read("W1", s)
                    b = big("W2", s)
                    nc.tensor.matmul(b[:, 0:n], W2[:, :], aggT[:, 0, 0:n], start=True, stop=True).then_inc(big_full, 1)
                    read("W2", s)
                    for j in range(nb):
                        b = sm("W3", s, j)
                        nc.tensor.matmul(b[:, 0:D], aggT[:, 1, j * P:(j + 1) * P], W3[:, :],
                                         start=True, stop=True).then_inc(sm_full, 1)
                elif kind in ("hidden0", "hidden1"):
                    if kind == "hidden0":
                        pe.wait_ge(n2_ready, s + 1)
                        turn("n2T", s, lambda j: n2[:, j, :])
                        read("n2T", s, KC - 1)
                    for c in chunks(kind):
                        b = big("F1", s, c)
                        for k in range(KC):
                            last = nc.tensor.matmul(b[:, 0:n], F1[:, k, c * P:(c + 1) * P], fT[:, k, 0:n],
                                                    start=(k == 0), stop=(k == KC - 1))
                        last.then_inc(big_full, 1)
                elif kind == "rank":
                    pe.wait_ge(diag_ready, 2 + s)
                    b = big("wrow", s)
                    for j in range(nb):
                        last = nc.tensor.matmul(b[:, j * P:(j + 1) * P], ones[:, :], diag[:, j, :], start=True, stop=True)
                    last.then_inc(big_full, 1)
                else:
                    read("F1", s, HC - 1)
                    for j in pieces(kind, s):
                        b = sm("F2", s, j)
                        for c in range(HC):
                            last = nc.tensor.matmul(b[:, 0:D], hT[:, c, j * P:(j + 1) * P], F2[:, c, :],
                                                    start=(c == 0), stop=(c == HC - 1))
                        last.then_inc(sm_full, 1)

            pe.wait_ge(plan_ready, 1)
            pos = pe.alloc_register("pe_pos")
            seen = pe.alloc_register("pe_seen")
            pe.reg_mov(pos, 1)
            pe.reg_mov(seen, 1)
            pe.sem_inc(released, RQ)
            pe.sem_inc(oh_used, OR)
            hot_seen = pe.alloc_register("pe_hot_seen")
            pe.reg_mov(hot_seen, 1)
            pe.sem_inc(hot_used[0], 1)
            pe.sem_inc(hot_used[1], 1)

            def visit(b, release):
                p = pe.snap(pos, min_val=1, max_val=NB * QP)
                v = pe.snap(seen, min_val=1, max_val=NB * QP + NB)
                oplace = pe.snap((v % OR) * (4 * P), min_val=0, max_val=(OR - 1) * 4 * P)
                place = pe.snap(((p - 1) % RQ) * (4 * W), min_val=0, max_val=(RQ - 1) * 4 * W)
                pe.wait_ge(landed, p)
                pe.wait_ge(oh_ready, v)
                for j in range(4):
                    mm = nc.tensor.matmul(AG[b % 2][:, :], onehot[:, ds(oplace + j * P, P)], ring[:, ds(place + j * W, W)],
                                          start=False, stop=False, skip_group_check=True)
                    if release and j == 0:
                        mm.then_inc(released, 1)
                mm.then_inc(oh_used, 1)
                pe.reg_add(seen, seen, 1)

            def segment(b, rest):
                row = 6 if rest else 2
                more = pe.value_load(plan[0:1, row, b:b + 1], min_val=0, max_val=QP)
                if not rest:
                    if b >= 2:
                        pe.wait_ge(agg_done, b - 1)
                    nc.tensor.matmul(AG[b % 2][:, :], zeros[:, 0:P], zeros[:, :], start=True, stop=False,
                                     skip_group_check=True)
                    visit(b, False)
                with pe.If(more > 0):
                    with pe.Fori(0, more):
                        pe.reg_add(pos, pos, 1)
                        visit(b, True)
                if rest:
                    nc.tensor.matmul(AG[b % 2][:, 0:2], zeros[:, 0:P], zeros[:, 0:2], start=False, stop=True,
                                     skip_group_check=True).then_inc(agg_full, 1)

            def count(g):
                visits = pe.value_load(plan[0:1, 5, g:g + 1], min_val=1, max_val=QP)
                b = big("counts", g)
                nc.tensor.matmul(b[:, 510:512], zeros[:, 0:P], zeros[:, 0:2], start=True, stop=False,
                                 skip_group_check=True)
                with pe.Fori(0, visits):
                    v = pe.snap(hot_seen, min_val=1, max_val=HG * QP + 1)
                    for h in range(2):
                        pe.wait_ge(hot_ready[h], v + h)
                        for j in (2 * h, 2 * h + 1):
                            mm = nc.tensor.matmul(b[:, 0:GC], oh_row[:, j, :], oh_key[:, j, :],
                                                  start=False, stop=False, skip_group_check=True)
                        mm.then_inc(hot_used[h], 1)
                    pe.reg_add(hot_seen, hot_seen, 1)
                nc.tensor.matmul(b[:, 510:512], zeros[:, 0:P], zeros[:, 0:2], start=False, stop=True,
                                 skip_group_check=True).then_inc(big_full, 1)

            def dense(k):
                if k == 0:
                    read("counts", HG - 1)
                banks = [BIG[at[("big", "hotT", c)] % 4] for c in range(KC)]
                if k == 0:
                    for c in range(KC):
                        big("hotT", c)
                pe.wait_ge(m_in[k % 2], 16 * (k // 2 + 1))
                for a in range(k * MK, min(k * MK + MK, A)):
                    for c in range(KC):
                        for part in range(2):
                            mm = nc.tensor.matmul(banks[c][:, 0:HOT * P],
                                                  mring[:, k % 2, a % MK, part * D + c * P:part * D + (c + 1) * P],
                                                  counts[:, a, 0:HOT * P], start=(a == 0 and part == 0),
                                                  stop=(a == A - 1 and part == 1))
                        if a == A - 1:
                            mm.then_inc(big_full, 1)
                        elif a % MK == MK - 1 and c == KC - 1:
                            mm.then_inc(m_used, 1)

            for kind, s in steps_of:
                if kind in ("visit", "more"):
                    segment(s, kind == "more")
                elif kind == "counts":
                    count(s)
                elif kind == "dense":
                    dense(s)
                elif kind != "tally":
                    phase(kind, s)

        @block.vector
        def _(dve):
            steps = [0]

            def step(ins):
                steps[0] += 1
                ins.then_inc(v_step, 1)
                dve.wait_ge(v_step, steps[0])

            def sm(*key):
                n = at[("sm",) + key]
                dve.wait_ge(sm_full, n + 1)
                return SM[n % 2]

            dve.wait_ge(consts, N_CONSTS - 1)
            nc.vector.tensor_scalar(ident[:, :], iota[:, :], pcol[:, :], None, ALU.is_equal).then_inc(consts, 1)
            nc.vector.tensor_scalar(before[:, :], iota[:, :], pcol[:, :], None, ALU.is_lt)

            dve.wait_ge(x_in, 16 * (len(range(0, NB - 1, 8)) + 1))
            for n, (a, z) in enumerate(((0, 4), (4, NB))):
                for t in range(a, z):
                    step(nc.vector.bn_stats(st[:, t % 4, :], X[:, t, :]))
                    last = nc.vector.bn_aggr(mv[:, t, :], st[:, t % 4, :])
                step(last)
                nc.vector.tensor_scalar(ve[:, a:z], mv[:, a:z, 1], EPS, None, ALU.add).then_inc(var_ready, 1)
                dve.wait_ge(std_ready, n + 1)
                step(nc.vector.reciprocal(rs[:, a:z], sd[:, a:z]))
                for s in range(0 if a == 0 else 1, 1 if a == 0 else NS):
                    for t in range(4 * s, 4 * s + blocks(s)):
                        last = nc.vector.tensor_scalar(Y[:, t, :], X[:, t, :], mv[:, t, 0:1], rs[:, t:t + 1],
                                                       ALU.subtract, ALU.mult)
                    last.then_inc(feat_ready, 1)
                if n == 0:
                    dve.wait_ge(weights_in, 16 * N_LOADS)
                    nc.vector.tensor_scalar(br_row[:, :], br_row[:, :], SCALE, None, ALU.mult)
                    nc.vector.tensor_scalar(br_col[:, :], br_col[:, :], SCALE, None, ALU.mult).then_inc(scaled, 1)

            dve.wait_ge(edges_in, 16 * N_EDGE_LOADS)
            nc.vector.tensor_copy(dst_f, dst_i)
            step(nc.vector.scalar_tensor_tensor(row_f, rel_i, float(NB * P), src_i, ALU.mult, ALU.add))
            step(nc.vector.tensor_reduce(tmm[:, 0, :], dst_f.rearrange("p (c e) -> p c e", c=TC), AX.X, ALU.min))
            nc.vector.tensor_reduce(tmm[:, 1, :], dst_f.rearrange("p (c e) -> p c e", c=TC), AX.X,
                                    ALU.max).then_inc(lists_ready, 1)
            dve.wait_ge(lists_ready, 1)
            dve.wait_ge(consts, N_CONSTS)
            for m in range(2):
                for c in range(TC):
                    last = nc.vector.tensor_scalar(diag_lists[:, m * TC + c, :], ident[:, :], tmm[:, m, c:c + 1], None, ALU.mult)
            last.then_inc(diag_ready, 1)

            def lows(s):
                for r in range(2):
                    k = 2 * s + r
                    for j in range(blocks(s)):
                        i = at[("sm", "L2", s, r, j)]
                        dve.wait_ge(hi_ready, sum(1 for x in sm_items[:i + 1] if x[0] == "L2"))
                        nc.vector.scalar_tensor_tensor(stage[:, k % 2, j, D:W], SM[i % 2][:, 0:D], 0.0,
                                                       stage[:, k % 2, j, 0:D], ALU.max,
                                                       ALU.subtract).then_inc(sm_free, 1)

            def make_plan():
                dve.wait_ge(big_free, at[("big", "spread", 3)] + 1)
                for k in range(HOT):
                    step(nc.vector.tensor_scalar(tmp, tmin_b, nodes[:, k:k + 1], None, ALU.is_le))
                    step(nc.vector.scalar_tensor_tensor(tmp, tmax_b, nodes[:, k:k + 1], tmp, ALU.is_ge, ALU.mult,
                                                        accum_out=tiles_of[:, k:k + 1]))
                nc.vector.tensor_reduce(rng[:, 2:3], tiles_of[:, :], AX.X, ALU.max)
                step(nc.vector.scalar_tensor_tensor(tmin_b, tmin_b, lo_g[:, 1:2], up, ALU.is_le, ALU.mult))
                nc.vector.tensor_reduce(rng[:, 1:2], tmin_b, AX.X, ALU.max)
                step(nc.vector.scalar_tensor_tensor(tmax_b, tmax_b, lo_g[:, 0:1], down, ALU.is_ge, ALU.mult))
                step(nc.vector.tensor_reduce(rng[:, 0:1], tmax_b, AX.X, ALU.max))
                nc.vector.tensor_scalar(rng[:, 0:1], rng[:, 0:1], -1.0, float(TW - 1), ALU.mult,
                                        ALU.add).then_inc(range_ready, 1)
                step(nc.vector.tensor_scalar(keys_i, rowT[:, :], P - 1, None, ALU.bitwise_and))
                nc.vector.tensor_copy(kb[:, :, 0], keys_i)
                nc.vector.tensor_scalar(dst16[:, :], dstT, float(CENTER), None, ALU.subtract)
                step(nc.vector.tensor_scalar(keys_i2, rowT[:, :], 7, None, ALU.arith_shift_right))
                nc.vector.scalar_tensor_tensor(kb[:, :, 1], dstT, float(A), keys_i2, ALU.mult,
                                               ALU.add).then_inc(keys_ready, 1)
                b = sm("ranges")
                step(nc.vector.tensor_reduce(okv[:, 38:39], b[0:1, 2 * P:3 * P], AX.X, ALU.max))
                step(nc.vector.tensor_copy(q_i[:, :], b[0:1, 0:2 * P]))
                dve.sem_inc(sm_free, 1)
                step(nc.vector.tensor_scalar(q_i[:, :], q_i[:, :], 2, None, ALU.arith_shift_right))
                step(nc.vector.tensor_copy(q_f[:, :], q_i[:, :]))
                step(nc.vector.tensor_tensor(okv[:, HOT:NB - 1], q0[:, HOT + 1:NB], q1[:, HOT:NB - 1], ALU.is_ge))
                step(nc.vector.tensor_scalar(okv[:, NB - 1:NB], okv[:, 38:39], float(MAX_TILES), None, ALU.is_le))
                step(nc.vector.tensor_reduce(okv[:, 39:40], okv[:, HOT:NB], AX.X, ALU.min))
                for row, v in enumerate((QP - 1, 0, 0, 1, QP - 1, 1)):
                    last = nc.vector.memset(pn[:, row, :], float(v))
                step(last)
                step(nc.vector.tensor_copy(pn[:, 0, HOT + 1:NB], q1[:, HOT:NB - 1]))
                step(nc.vector.tensor_tensor(pn[:, 0, HOT:HOT + 1], q0[:, HOT:HOT + 1], q1[:, HOT:HOT + 1], ALU.min))
                nc.vector.tensor_scalar(pn[:, 1, HOT:NB], pn[:, 0, HOT:NB], 1.0, None, ALU.add)
                nc.vector.tensor_copy(pn[:, 3, 1:2], pn[:, 0, HOT:HOT + 1])
                nc.vector.tensor_copy(pn[:, 4, 0:HG], h0[:, 0:HG])
                nc.vector.tensor_tensor(pn[:, 2, HOT:NB], q1[:, HOT:NB], pn[:, 0, HOT:NB], ALU.subtract)
                step(nc.vector.scalar_tensor_tensor(pn[:, 5, 0:HG], h1[:, 0:HG], 1.0, h0[:, 0:HG], ALU.add, ALU.subtract))
                step(nc.vector.tensor_scalar(pn[:, 5, 0:HG], pn[:, 5, 0:HG], 1.0, None, ALU.max))
                step(nc.vector.scalar_tensor_tensor(pn[:, 3, 0:1], q1[:, NB - 1:NB], 1.0, pn[:, 0, HOT:HOT + 1], ALU.add,
                                                    ALU.subtract))
                step(nc.vector.tensor_tensor(pn[:, :, :], pn[:, :, :], pf[:, :, :], ALU.subtract))
                step(nc.vector.scalar_tensor_tensor(pn[:, :, :], pn[:, :, :], okv[:, 39:40], pf[:, :, :], ALU.mult,
                                                    ALU.add))
                step(nc.vector.tensor_copy(plan[:, 0:6, :], pn[:, :, :]))
                step(nc.vector.tensor_scalar(plan[:, 6, :], plan[:, 2, :], 1, None, ALU.arith_shift_right))
                step(nc.vector.tensor_tensor(plan[:, 2, :], plan[:, 2, :], plan[:, 6, :], ALU.subtract))
                nc.vector.tensor_tensor(plan[:, 7, :], plan[:, 1, :], plan[:, 2, :], ALU.add).then_inc(plan_ready, 1)

            for s in range(NS):
                lows(s)
                if s == 1:
                    make_plan()
            dve.wait_ge(weights_in, 16 * N_LOADS)
            for t in range(NB):
                nc.vector.tensor_tensor(X[:, t, :], X[:, t, :], b3[:, :], ALU.add)
            nc.vector.tensor_tensor(bg[:, :], bi[:, :], bh[:, :], ALU.add).then_inc(bias_ready, 1)

            def norm2(s):
                nb = blocks(s)
                t0 = 4 * s
                for j in range(nb):
                    b = sm("W3", s, j)
                    step(nc.vector.tensor_tensor(X[:, t0 + j, :], X[:, t0 + j, :], b[:, 0:D], ALU.add))
                    dve.sem_inc(sm_free, 1)
                    step(nc.vector.bn_stats(st[:, j, :], X[:, t0 + j, :]))
                    last = nc.vector.bn_aggr(mv[:, t0 + j, :], st[:, j, :])
                step(last)
                nc.vector.tensor_scalar(ve[:, t0:t0 + nb], mv[:, t0:t0 + nb, 1], EPS, None, ALU.add).then_inc(var_ready, 1)
                dve.wait_ge(std_ready, 3 + s)
                step(nc.vector.reciprocal(rs[:, t0:t0 + nb], sd[:, t0:t0 + nb]))
                for j in range(nb):
                    t = t0 + j
                    last = nc.vector.tensor_scalar(n2[:, j, :], X[:, t, :], mv[:, t, 0:1], rs[:, t:t + 1],
                                                   ALU.subtract, ALU.mult)
                last.then_inc(n2_ready, 1)
                dve.wait_ge(n2_ready, s + 1)
                for j in range(nb):
                    t = t0 + j
                    nc.vector.tensor_tensor(X[:, t, :], X[:, t, :], n2[:, j, :], ALU.add)
                    nc.vector.tensor_tensor_reduce(out=junk[:, j * D:(j + 1) * D], in0=n2[:, j, :], in1=wr[:, :], scale=1.0,
                                                   scalar=0.0, op0=ALU.mult, op1=ALU.add,
                                                   accum_out=wcol[:, t:t + 1]).then_inc(v_step, 1)
                steps[0] += nb
                dve.wait_ge(v_step, steps[0])
                step(nc.vector.tensor_scalar(wcol[:, t0:t0 + nb], wcol[:, t0:t0 + nb], br[:, :], None, ALU.add))

            def phase(kind, s):
                n = blocks(s) * P
                if kind == "gates":
                    if s == 0:
                        dve.wait_ge(big_free, at[("big", "aggT", s, KC - 1)] + 1)
                        nc.vector.tensor_tensor(aggT[:, :, 0:HOT * P], aggT[:, :, 0:HOT * P], fT[:, :, 0:HOT * P],
                                                ALU.add).then_inc(hot_added, 1)
                    dve.wait_ge(big_free, at[("big", "gate", s, 3)] + 1)
                    nc.vector.tensor_tensor(G[:, 0:2, 0:n], G[:, 0:2, 0:n], G[:, 2:4, 0:n], ALU.mult).then_inc(c_ready, 1)
                    dve.wait_ge(tc_ready, s + 1)
                    dve.wait_ge(big_free, at[("big", "gate", s, 5)] + 1)
                    nc.vector.tensor_tensor(hnT[:, :, 0:n], G[:, 4:6, 0:n], G[:, 2:4, 0:n], ALU.mult).then_inc(hn_ready, 1)
                elif kind == "mlp":
                    norm2(s)
                elif kind == "rank":
                    ranks(s)
                elif kind in ("down0", "down1"):
                    for j in pieces(kind, s):
                        b = sm("F2", s, j)
                        nc.vector.tensor_tensor(Y[:, 4 * s + j, :], b[:, 0:D], fb2[:, :], ALU.add).then_inc(sm_free, 1)

            seen = dve.alloc_register("dve_seen")
            dve.reg_mov(seen, 1)
            col = dve.alloc_register("dve_col")

            def ranks(s):
                nb = blocks(s)
                for j in range(nb):
                    last = nc.vector.tensor_scalar(diag[:, j, :], ident[:, :], wcol[:, 4 * s + j:4 * s + j + 1], None, ALU.mult)
                last.then_inc(diag_ready, 1)

            def tally(s, lo_t, hi_t):
                dve.wait_ge(big_free, at[("big", "wrow", s)] + 1)
                start, end = 4 * s * P, min(4 * s * P + blocks(s) * P, N)

                def count(t, k, lo, hi, op):
                    if hi > lo:
                        step(nc.vector.tensor_scalar(junk[:, 0:hi - lo], w_all[:, lo:hi], wcol[:, t:t + 1], None, op,
                                                     ALU.add, accum_out=rank4[:, t, k:k + 1]))
                for t in range(lo_t, hi_t):
                    if t < 4 * s:
                        count(t, 3 + s, start, end, ALU.is_gt)
                    else:
                        a, z = t * P, min(t * P + P, N)
                        count(t, 0, 0, min(a, NB * P // 2), ALU.is_ge)
                        count(t, 3 + NS, NB * P // 2, a, ALU.is_ge)
                        count(t, 1, a, end, ALU.is_gt)
                        step(nc.vector.scalar_tensor_tensor(junk[:, 0:z - a], w_all[:, a:z], wcol[:, t:t + 1], before[:, 0:z - a],
                                                            ALU.is_equal, ALU.mult, accum_out=rank4[:, t, 2:3]))

            hot_seen = dve.alloc_register("dve_hot_seen")
            dve.sem_inc(hot_ready[1], 1)
            dve.reg_mov(hot_seen, 1)

            def count_visits(g):
                q = dve.value_load(plan[0:1, 4, g:g + 1], min_val=0, max_val=QP - 1)
                visits = dve.value_load(plan[0:1, 5, g:g + 1], min_val=1, max_val=QP)
                dve.reg_mul(col, q, 4)
                with dve.Fori(0, visits):
                    v = dve.snap(hot_seen, min_val=1, max_val=HG * QP + 1)
                    c = dve.snap(col, min_val=0, max_val=4 * QP)
                    dve.wait_ge(hot_ready[1], v)
                    nc.vector.tensor_copy(kb4[:, :, :], kb[:, ds(c, 4), :]).then_inc(kb_ready, 1)
                    dve.wait_ge(kb_ready, v)
                    for h in range(2):
                        dve.wait_ge(hot_used[h], v)
                        for j in (2 * h, 2 * h + 1):
                            nc.vector.tensor_scalar(oh_row[:, j, :], iota16[:, 0:P], kb4[:, j, 0:1], None, ALU.is_equal)
                            last = nc.vector.tensor_scalar(oh_key[:, j, :], iota16[:, 0:GC], kb4[:, j, 1:2],
                                                           float(-g * GC), ALU.subtract, ALU.is_equal)
                        last.then_inc(hot_ready[h], 1)
                    dve.reg_add(hot_seen, hot_seen, 1)
                    dve.reg_add(col, col, 4)

            def visit(b):
                v = dve.snap(seen, min_val=1, max_val=NB * QP + NB)
                c = dve.snap(col, min_val=0, max_val=4 * QP)
                place = dve.snap((v % OR) * (4 * P), min_val=0, max_val=(OR - 1) * 4 * P)
                dve.wait_ge(oh_used, v)
                nc.vector.tensor_tensor(onehot[:, ds(place, 4 * P)].rearrange("p (t n) -> p t n", n=P),
                                        dst16[:, ds(c, 4)].unsqueeze(2).broadcast_to([P, 4, P]),
                                        iota_b[:, b % 2, :].unsqueeze(1).broadcast_to([P, 4, P]),
                                        ALU.is_equal).then_inc(oh_ready, 1)
                dve.reg_add(seen, seen, 1)

            def nodes_of(b):
                if b < NB:
                    nc.vector.tensor_scalar(iota_b[:, b % 2, :], iota16[:, 0:P], float(b * P - CENTER), None,
                                            ALU.add).then_inc(nodes_ready, 1)

            def segment(b, rest):
                row = 6 if rest else 2
                if not rest:
                    q = dve.value_load(plan[0:1, 0, b:b + 1], min_val=0, max_val=QP - 1)
                    dve.reg_mul(col, q, 4)
                    dve.wait_ge(nodes_ready, b + 1)
                    visit(b)
                q2 = dve.value_load(plan[0:1, 7 if rest else 1, b:b + 1], min_val=0, max_val=QP)
                more = dve.value_load(plan[0:1, row, b:b + 1], min_val=0, max_val=QP)
                dve.reg_mul(col, q2, 4)
                with dve.If(more > 0):
                    with dve.Fori(0, more):
                        visit(b)
                        dve.reg_add(col, col, 4)
                if not rest:
                    close()
                    nodes_of(b + 1)
                    open_block.append(b)

            open_block = []

            def close():
                while open_block:
                    b = open_block.pop()
                    dve.wait_ge(agg_copied, b + 1)
                    if b % 4 == 0 and b >= AB:
                        dve.wait_ge(big_full, at[("big", "aggT", (b - AB) // 4, KC - 1)] + 1)
                    nc.vector.scalar_tensor_tensor(agg[:, b % AB, :], AG[b % 2][:, D:W], 1 / SCALE, agg_hi[:, :], ALU.mult,
                                                   ALU.add).then_inc(agg_done, 1)

            nodes_of(0)
            step(nc.vector.memset(rank4[:, :, :], 0.0))
            for kind, s in steps_of:
                if kind == "gates" and open_block and open_block[0] < 4 * s + blocks(s):
                    close()
                if kind in ("visit", "more"):
                    segment(s, kind == "more")
                elif kind == "counts":
                    count_visits(s)
                elif kind == "tally":
                    tally(*s)
                elif kind != "dense":
                    phase(kind, s)

            step(nc.vector.tensor_reduce(rank[:, :], rank4[:, :, :], AX.X, ALU.add))
            step(nc.vector.scalar_tensor_tensor(mw[:, :], rank[:, :], float(NSEL), wcol[:, :], ALU.is_lt, ALU.mult))
            for t in range(NB):
                nc.vector.scalar_tensor_tensor(X[:, t, :], Y[:, t, :], mw[:, t:t + 1], X[:, t, :], ALU.mult,
                                               ALU.add).then_inc(out_ready, 1)


N_LOADS = 18
N_EDGE_LOADS = 9
N_CONSTS = 24


def kernel(**inputs):
    import numpy as np
    import concourse.bacc as bacc
    from concourse.bass_utils import run_bass_kernel_spmd

    a = {k: np.asarray(v) for k, v in inputs.items()}
    D = a["x"].shape[1]

    def gates(w):
        return np.concatenate([w[0:D], w[2 * D:3 * D], w[3 * D:4 * D]])

    def cols(v):
        return v.reshape(-1, P).T

    laid = {
        "x": a["x"], "src": a["src"], "dst": a["dst"], "rel": a["edge_type_2"],
        "w_rel_t": a["L0_gnn_W_rel"].transpose(0, 2, 1),
        "b_rel_col": cols(a["L0_gnn_b_rel"]), "b_rel_row": a["L0_gnn_b_rel"].reshape(1, -1),
        "w_ih_t": gates(a["L0_gnn_W_ih"]).T, "b_ih_col": cols(gates(a["L0_gnn_b_ih"])),
        "b_hh_col": cols(gates(a["L0_gnn_b_hh"])),
        "w1_t": a["L0_gnn_W1"].T, "b1_col": cols(a["L0_gnn_b1"]),
        "w2_t": a["L0_gnn_W2"].T, "b2_col": cols(a["L0_gnn_b2"]),
        "w3_t": a["L0_gnn_W3"].T, "b3_row": a["L0_gnn_b3"].reshape(1, -1),
        "wr_row": a["L0_ffn_wr"].reshape(1, -1), "br_one": a["L0_ffn_br"].reshape(1, 1),
        "f1": a["L0_ffn_w1"], "f1_col": cols(a["L0_ffn_b1"]), "f2": a["L0_ffn_w2"],
        "f2_row": a["L0_ffn_b2"].reshape(1, -1),
    }
    nc = bacc.Bacc("TRN2", target_bir_lowering=False, num_devices=1)
    arrays, args = {}, []
    for name, v in laid.items():
        v = np.ascontiguousarray(v)
        arrays[f"in_{name}"] = v
        args.append(nc.dram_tensor(f"in_{name}", v.shape, mybir.dt.from_np(v.dtype), kind="ExternalInput").ap())
    args.append(nc.dram_tensor("out", a["x"].shape, F32, kind="ExternalOutput").ap())
    build(nc, *args)
    r = run_bass_kernel_spmd(nc, [arrays], core_ids=[0])
    return r.results[0]["out"]
```
